# Optimizing a Trainium2 kernel written in Bass

```python
import numpy as np
import jax
import jax.numpy as jnp

def _softmax(x, axis=-1):
    return jax.nn.softmax(x, axis=axis)

def _gelu(x):
    return jax.nn.gelu(x, approximate=True)

def _silu(x):
    return jax.nn.silu(x)

def _sigmoid(x):
    return jax.nn.sigmoid(x)

def _layernorm(x, axis=-1, eps=1e-05):
    m = jnp.mean(x, axis=axis, keepdims=True)
    v = jnp.var(x, axis=axis, keepdims=True)
    return (x - m) / jnp.sqrt(v + eps)

def _scatter_add(tgt, idx, src, axis=0):
    return tgt.at[idx].add(src)

def _segment_sum(src, seg, n):
    return jax.ops.segment_sum(src, seg, n)
kernel_name = 'mk_gnn_resnorm_d2_gnn_r8_8e4340'

def setup_inputs(seed: int=0):
    np.random.seed(seed)
    _w = jnp.asarray

    def _rec_inputs():
        import jax
        import jax.numpy as jnp
        _gk = jax.random.key(seed)
        x = -0.0003713 + 1 * jax.random.normal(jax.random.fold_in(_gk, 1), (6250, 256), jnp.float32)
        _s = jax.random.randint(jax.random.fold_in(_gk, 2), (50000,), 0, 6250, jnp.int32)
        _d = jax.random.randint(jax.random.fold_in(_gk, 3), (50000,), 0, 6250, jnp.int32)
        _loop = jnp.arange(6250, dtype=jnp.int32)
        src = jnp.concatenate([_s, _d, _loop])
        dst = jnp.concatenate([_d, _s, _loop])
        _o = jnp.argsort(dst, stable=True)
        src = src[_o]
        dst = dst[_o]
        edge_attr_256 = 5.93493e-05 + 1.00006 * jax.random.normal(jax.random.fold_in(_gk, 11), (106250, 256), jnp.float32)
        return (x, src, dst, edge_attr_256)
    x, src, dst, edge_attr_256 = _rec_inputs()

    def _L0_gnn_setup():
        import jax, jax.numpy as jnp
        import numpy as np
        N, E, D = (6250, 37500, 256)
        BN_EPS = 1e-05

        def _bn(z, gamma, beta, mean, var):
            return (z - mean) * jax.lax.rsqrt(var + BN_EPS) * gamma + beta
        key = jax.random.key(seed)
        ks = jax.random.split(key, 8)
        s = 1.0 / np.sqrt(D)
        return {'x': jax.random.normal(ks[0], (N, D), dtype=jnp.float32), 'edge_index': jax.random.randint(ks[1], (2, E), 0, N, dtype=jnp.int64), 'edge_attr': jax.random.normal(ks[2], (E, D), dtype=jnp.float32), 'W1': jax.random.normal(ks[3], (D, D), dtype=jnp.float32) * s, 'b1': jnp.zeros((D,), jnp.float32), 'W2': jax.random.normal(ks[4], (D, D), dtype=jnp.float32) * s, 'b2': jnp.zeros((D,), jnp.float32), 'bn1_gamma': jnp.ones((D,), jnp.float32), 'bn1_beta': jnp.zeros((D,), jnp.float32), 'bn1_mean': jnp.zeros((D,), jnp.float32), 'bn1_var': jnp.ones((D,), jnp.float32), 'bn2_gamma': jnp.ones((D,), jnp.float32), 'bn2_beta': jnp.zeros((D,), jnp.float32), 'bn2_mean': jnp.zeros((D,), jnp.float32), 'bn2_var': jnp.ones((D,), jnp.float32)}
    _L0_gnn_all = _L0_gnn_setup()
    _L0_gnn_in = {k: v for k, v in _L0_gnn_all.items() if k in ('W1', 'b1', 'W2', 'b2', 'bn1_gamma', 'bn1_beta', 'bn1_mean', 'bn1_var', 'bn2_gamma', 'bn2_beta', 'bn2_mean', 'bn2_var')}
    del _L0_gnn_all

    def _L1_gnn_setup():
        import jax, jax.numpy as jnp
        import numpy as np
        N, E, D = (2500, 40000, 256)
        EPS = 1e-05

        def _layer_norm(x, gamma, beta):
            mu = jnp.mean(x, axis=-1, keepdims=True)
            var = jnp.mean(jnp.square(x - mu), axis=-1, keepdims=True)
            return (x - mu) * jax.lax.rsqrt(var + EPS) * gamma + beta
        key = jax.random.key(seed)
        ks = jax.random.split(key, 12)
        s = 1.0 / np.sqrt(D)
        s2 = 1.0 / np.sqrt(2 * D)
        return {'node_embeddings': jax.random.normal(ks[0], (N, D), jnp.float32), 'edge_index': jax.random.randint(ks[1], (2, E), 0, N, jnp.int64), 'edge_embeddings': jax.random.normal(ks[2], (E, D), jnp.float32), 'W1m': jax.random.uniform(ks[3], (D, D), jnp.float32, -s, s), 'b1m': jnp.zeros((D,), jnp.float32), 'W2m': jax.random.uniform(ks[4], (D, D), jnp.float32, -s, s), 'b2m': jnp.zeros((D,), jnp.float32), 'W1u': jax.random.uniform(ks[5], (D, 2 * D), jnp.float32, -s, s), 'b1u': jnp.zeros((2 * D,), jnp.float32), 'W2u': jax.random.uniform(ks[6], (2 * D, D), jnp.float32, -s2, s2), 'b2u': jnp.zeros((D,), jnp.float32), 'gamma': jnp.ones((D,), jnp.float32), 'beta': jnp.zeros((D,), jnp.float32)}
    _L1_gnn_all = _L1_gnn_setup()
    _L1_gnn_in = {k: v for k, v in _L1_gnn_all.items() if k in ('W1m', 'b1m', 'W2m', 'b2m', 'W1u', 'b1u', 'W2u', 'b2u', 'gamma', 'beta')}
    del _L1_gnn_all
    return {'x': x, 'src': src, 'dst': dst, 'edge_attr_256': edge_attr_256, 'L0_gnn_W1': _L0_gnn_in['W1'], 'L0_gnn_b1': _L0_gnn_in['b1'], 'L0_gnn_W2': _L0_gnn_in['W2'], 'L0_gnn_b2': _L0_gnn_in['b2'], 'L0_gnn_bn1_gamma': _L0_gnn_in['bn1_gamma'], 'L0_gnn_bn1_beta': _L0_gnn_in['bn1_beta'], 'L0_gnn_bn1_mean': _L0_gnn_in['bn1_mean'], 'L0_gnn_bn1_var': _L0_gnn_in['bn1_var'], 'L0_gnn_bn2_gamma': _L0_gnn_in['bn2_gamma'], 'L0_gnn_bn2_beta': _L0_gnn_in['bn2_beta'], 'L0_gnn_bn2_mean': _L0_gnn_in['bn2_mean'], 'L0_gnn_bn2_var': _L0_gnn_in['bn2_var'], 'L1_gnn_W1m': _L1_gnn_in['W1m'], 'L1_gnn_b1m': _L1_gnn_in['b1m'], 'L1_gnn_W2m': _L1_gnn_in['W2m'], 'L1_gnn_b2m': _L1_gnn_in['b2m'], 'L1_gnn_W1u': _L1_gnn_in['W1u'], 'L1_gnn_b1u': _L1_gnn_in['b1u'], 'L1_gnn_W2u': _L1_gnn_in['W2u'], 'L1_gnn_b2u': _L1_gnn_in['b2u'], 'L1_gnn_gamma': _L1_gnn_in['gamma'], 'L1_gnn_beta': _L1_gnn_in['beta']}

def reference(x, src, dst, edge_attr_256, L0_gnn_W1, L0_gnn_b1, L0_gnn_W2, L0_gnn_b2, L0_gnn_bn1_gamma, L0_gnn_bn1_beta, L0_gnn_bn1_mean, L0_gnn_bn1_var, L0_gnn_bn2_gamma, L0_gnn_bn2_beta, L0_gnn_bn2_mean, L0_gnn_bn2_var, L1_gnn_W1m, L1_gnn_b1m, L1_gnn_W2m, L1_gnn_b2m, L1_gnn_W1u, L1_gnn_b1u, L1_gnn_W2u, L1_gnn_b2u, L1_gnn_gamma, L1_gnn_beta):
    import jax
    import jax.numpy as jnp

    def _L0_gnn_ref(x, edge_index, edge_attr, W1, b1, W2, b2, bn1_gamma, bn1_beta, bn1_mean, bn1_var, bn2_gamma, bn2_beta, bn2_mean, bn2_var):
        import jax, jax.numpy as jnp
        import numpy as np
        N, E, D = (6250, 37500, 256)
        BN_EPS = 1e-05

        def _bn(z, gamma, beta, mean, var):
            return (z - mean) * jax.lax.rsqrt(var + BN_EPS) * gamma + beta
        src, dst = (edge_index[0], edge_index[1])
        msg = jax.nn.relu(x[src] + edge_attr)
        agg = jax.ops.segment_sum(msg, dst, num_segments=x.shape[0])
        conv_out = x + agg
        h = x + conv_out
        f = _bn(h, bn1_gamma, bn1_beta, bn1_mean, bn1_var)
        f = jax.nn.gelu(f @ W1.T + b1, approximate=False)
        f = f @ W2.T + b2
        return _bn(h + f, bn2_gamma, bn2_beta, bn2_mean, bn2_var)

    def _L1_gnn_ref(node_embeddings, edge_index, edge_embeddings, W1m, b1m, W2m, b2m, W1u, b1u, W2u, b2u, gamma, beta):
        import jax, jax.numpy as jnp
        import numpy as np
        N, E, D = (2500, 40000, 256)
        EPS = 1e-05

        def _layer_norm(x, gamma, beta):
            mu = jnp.mean(x, axis=-1, keepdims=True)
            var = jnp.mean(jnp.square(x - mu), axis=-1, keepdims=True)
            return (x - mu) * jax.lax.rsqrt(var + EPS) * gamma + beta
        src = edge_index[0]
        dst = edge_index[1]
        n = node_embeddings.shape[0]
        h = node_embeddings[src] + edge_embeddings
        h = jax.nn.gelu(h @ W1m + b1m, approximate=False)
        messages = h @ W2m + b2m
        agg = jax.ops.segment_sum(messages, dst, num_segments=n)
        deg = jax.ops.segment_sum(jnp.ones((dst.shape[0], 1), node_embeddings.dtype), dst, num_segments=n)
        agg = agg / jnp.maximum(deg, 1.0)
        u = jax.nn.gelu(agg @ W1u + b1u, approximate=False) @ W2u + b2u
        return _layer_norm(node_embeddings + u, gamma, beta)
    edge_index = jnp.stack([src, dst])
    x = _layernorm(x + _L0_gnn_ref(x, edge_index, edge_attr_256, L0_gnn_W1, L0_gnn_b1, L0_gnn_W2, L0_gnn_b2, L0_gnn_bn1_gamma, L0_gnn_bn1_beta, L0_gnn_bn1_mean, L0_gnn_bn1_var, L0_gnn_bn2_gamma, L0_gnn_bn2_beta, L0_gnn_bn2_mean, L0_gnn_bn2_var), axis=-1)
    x = _layernorm(x + _L1_gnn_ref(x, edge_index, edge_attr_256, L1_gnn_W1m, L1_gnn_b1m, L1_gnn_W2m, L1_gnn_b2m, L1_gnn_W1u, L1_gnn_b1u, L1_gnn_W2u, L1_gnn_b2u, L1_gnn_gamma, L1_gnn_beta), axis=-1)
    return x

_drawn_inputs = setup_inputs


def setup_inputs(seed=0):
    import zlib

    import numpy as np

    out = dict(_drawn_inputs(seed))
    spreads = {'L0_gnn_b1': (0.0, 0.8),
     'L0_gnn_b2': (0.0, 0.633),
     'L0_gnn_bn1_gamma': (1.0, 0.2),
     'L0_gnn_bn1_beta': (0.0, 0.8),
     'L0_gnn_bn1_mean': (0.0, 0.8),
     'L0_gnn_bn1_var': (1.0, 0.2),
     'L0_gnn_bn2_gamma': (1.0, 0.2),
     'L0_gnn_bn2_beta': (0.0, 0.789),
     'L0_gnn_bn2_mean': (0.0, 0.692),
     'L0_gnn_bn2_var': (1.0, 0.2),
     'L1_gnn_b1m': (0.0, 0.8),
     'L1_gnn_b2m': (0.0, 0.8),
     'L1_gnn_b1u': (0.0, 0.531),
     'L1_gnn_b2u': (0.0, 0.304),
     'L1_gnn_gamma': (1.0, 0.2),
     'L1_gnn_beta': (0.0, 0.1)}
    factors = {'L1_gnn_W1m': 4.119, 'L1_gnn_W2m': 2.903, 'L1_gnn_W1u': 2.812}
    for name, (base, spread) in spreads.items():
        noise = np.random.default_rng([zlib.crc32(name.encode()), seed]).standard_normal(out[name].shape)
        drawn = base * np.exp(spread * noise) if base else spread * noise
        out[name] = jnp.asarray(drawn.astype(out[name].dtype))
    for name, factor in factors.items():
        out[name] = (out[name] * factor).astype(out[name].dtype)
    return out
```

```python
from contextlib import ExitStack

import numpy as np

import concourse.bass as bass
from concourse import mybir

ALU = mybir.AluOpType
ACT = mybir.ActivationFunctionType
AX_X = mybir.AxisListType.X
F32 = mybir.dt.float32
I32 = mybir.dt.int32

P = 128
D = 256
KD = D // P
TILES = 6
PAIRS = TILES // 2
GROUP = TILES * P
WIN = 64
RING = 4
CHUNK = 256
BLK = CHUNK // P
STEPS = 4
EPS = 1e-5
OUTSIDE = -1.0e6

VT = ["L0_b1", "L0_b2", "bn1_gamma", "bn1_beta", "bn1_mean", "bn1_var",
      "bn2_gamma", "bn2_beta", "bn2_mean", "bn2_var", "b2m", "b2u", "b1u_lo", "b1u_hi"]
VR = ["b1m", "gamma", "beta"]


class Step:

    def __init__(self, i, phase, chunks, nodes):
        self.i, self.phase, self.chunks, self.nodes = i, phase, chunks, nodes

    def at(self, offset):
        c = self.i - offset
        if isinstance(self.i, int):
            if not 0 <= c < self.chunks:
                return None
            return c, min(c * CHUNK, self.nodes - CHUNK), c % STEPS
        return c, c * CHUNK, (self.phase - offset) % STEPS


def run_steps(eng, body, chunks, nodes, depth):
    first = 2 * STEPS
    rounds = max(0, (chunks - 1 - first) // STEPS)
    for i in range(min(first, chunks + depth)):
        body(Step(i, i % STEPS, chunks, nodes))
    if rounds:
        with eng.Fori(0, rounds) as r:
            for s in range(STEPS):
                body(Step(r * STEPS + (first + s), s, chunks, nodes))
    for i in range(first + rounds * STEPS, chunks + depth):
        body(Step(i, i % STEPS, chunks, nodes))


def run_groups(eng, body, start, stop):
    rounds = (stop - start) // RING
    if rounds:
        with eng.Fori(0, rounds) as r:
            for s in range(RING):
                body(r * RING + (start + s), (start + s) % RING)
    for g in range(start + rounds * RING, stop):
        body(g, g % RING)


def build(nc, x, xT, src, dst, edge, w1T, w2T, w1m, w2m, w1u, w2u, vt, vr, out):
    N = x.shape[0]
    E = edge.shape[0]
    full = E // GROUP
    G = -(-E // GROUP)
    repeated = G * GROUP - E
    NW = -(-N // WIN)
    NPAD = N + WIN
    C = -(-N // CHUNK)
    H2 = w1u.shape[1]
    KH = H2 // P
    assert RING < full and G <= 512 and C >= 2 and KH == 2 * KD

    y_dram = nc.dram_tensor("y_scratch", [N, D], F32, kind="Internal").ap()
    x1_dram = nc.dram_tensor("x1_scratch", [N, D], F32, kind="Internal").ap()
    x1T_dram = nc.dram_tensor("x1T_scratch", [D, N], F32, kind="Internal").ap()

    with ExitStack() as ctx:
        def sb(name, shape, dt=F32):
            return ctx.enter_context(nc.sbuf_tensor(name, shape, dt))

        def sem(name):
            return ctx.enter_context(nc.semaphore(name))

        def sems(name, n):
            return [sem(f"{name}{i}") for i in range(n)]

        bank = [ctx.enter_context(nc.psum_tensor(f"bank{i}", [P, 512], F32)) for i in range(8)]

        acc = sb("acc", [P, KD + 1, NPAD])
        e_sb = [sb(f"e{s}", [P, TILES, D]) for s in range(RING)]
        m_all = sb("m_all", [P, RING * TILES * D])
        m_sb = [m_all[:, s * TILES * D:(s + 1) * TILES * D].rearrange("p (u d) -> p u d", d=D)
                for s in range(RING)]
        src_sb = [sb(f"src{s}", [P, TILES], I32) for s in range(RING)]
        eT_sb = [sb(f"eT{s}", [P, PAIRS, 512]) for s in range(2)]
        sel = [sb(f"sel{s}", [P, TILES, WIN]) for s in range(2)]
        dst_i = sb("dst_i", [P, G, TILES], I32)
        dst_f = sb("dst_f", [P, G, TILES])
        rel = sb("rel", [P, G, TILES])
        win_i = sb("win_i", [1, G], I32)
        win_f = sb("win_f", [1, G])
        win_bc = sb("win_bc", [P, G])
        iota_i = sb("iota_i", [P, WIN], I32)
        iota = sb("iota", [P, WIN])
        place_i = sb("place_i", [P, TILES], I32)
        repeat = sb("repeat", [P, TILES])
        extent = sb("extent", [P, 4])
        general = sb("general", [P, 1], I32)
        rel_k = sb("rel_k", [P, TILES])
        ones = sb("ones", [P, P])
        ident = sb("ident", [P, P])
        root = sb("root", [P, BLK])
        eps_t = sb("eps_t", [P, BLK])
        w1T_sb = sb("w1T_sb", [P, KD, D])
        w2T_sb = sb("w2T_sb", [P, KD, D])
        w1m_sb = sb("w1m_sb", [P, KD, D])
        w2m_sb = sb("w2m_sb", [P, KD, D])
        w1u_sb = sb("w1u_sb", [P, KD, H2])
        w2u_sb = sb("w2u_sb", [P, KH, D])
        vt_sb = sb("vt_sb", [P, len(VT), KD])
        vr_sb = sb("vr_sb", [P, len(VR), D])
        bn_r = sb("bn_r", [P, 2, KD])
        bn_s = sb("bn_s", [P, 2, KD])
        bn_c = sb("bn_c", [P, 2, KD])
        bn_t = sb("bn_t", [P, 2, KD])

        def vec(name, k):
            return vt_sb[:, VT.index(name), k:k + 1]

        def row(name):
            return vr_sb[:, VR.index(name), :].unsqueeze(1).broadcast_to([P, BLK, D])

        UNIT = KD * CHUNK

        def spare(first, n, inner=CHUNK):
            return [m_all[:, (first + i) * UNIT:(first + i + 1) * UNIT].rearrange("p (k n) -> p k n", n=inner)
                    for i in range(n)]

        h_n = spare(0, 4)
        xc_n = spare(4, 4)
        u_n = spare(8, 2)
        y_n = spare(10, 2, D)
        q_n = spare(0, 2)
        r_n = spare(2, 2)
        xb_n = spare(4, 4, D)
        n_n = spare(8, 2, D)
        o_n = spare(10, 2, D)
        xt_n = [sb(f"xt_n{i}", [P, KD, CHUNK]) for i in range(2)]
        f_n = [sb(f"f_n{i}", [P, KD, CHUNK]) for i in range(2)]
        x1_n = [sb(f"x1_n{i}", [P, BLK, D]) for i in range(2)]
        g_n = [sb(f"g_n{i}", [P, KH, CHUNK]) for i in range(2)]
        x1T_n = [g_n[i][:, KD:KH, :] for i in range(2)]
        st_n = [sb(f"st_n{i}", [P, 2, BLK, 6]) for i in range(2)]
        mv_n = [sb(f"mv_n{i}", [P, 2, BLK, 2]) for i in range(2)]
        rs_n = [sb(f"rs_n{i}", [P, 2, BLK]) for i in range(2)]

        dst_in = sem("dst_in")
        consts_in = sem("consts_in")
        consts_made = sem("consts_made")
        prep = sem("prep")
        win_ready = sem("win_ready")
        win_spread = sem("win_spread")
        extent_ready = sem("extent_ready")
        counted = sem("counted")
        general_made = sem("general_made")
        var_made = sem("var_made")
        root_made = sem("root_made")
        bn_made = sem("bn_made")
        e_in = sems("e_in", RING)
        src_in = sems("src_in", RING)
        m_in = sems("m_in", RING)
        gather_go = sem("gather_go")
        e_read = sem("e_read")
        added = sem("added")
        msg_made = sem("msg_made")
        sel_made = sem("sel_made")
        seg_done = sem("seg_done")
        acc_done = sem("acc_done")
        gen_go = sem("gen_go")
        gen_rel = sem("gen_rel")
        gen_sel = sem("gen_sel")
        gen_seg = sem("gen_seg")
        gen_acc = sem("gen_acc")
        turned = sem("turned")
        eT_made = sem("eT_made")
        z_made = sem("z_made")
        z_added = sem("z_added")
        gelu_made = sem("gelu_made")
        waited = {e: sem(f"waited_{e.name}") for e in (nc.sync.engine, nc.vector.engine)}
        acc_zero = sem("acc_zero")

        (a_h, a_xc, a_f, a_z1, a_g, a_z2, a_t, a_u, a_uT, a_st, a_mv, a_ve, a_rs, a_x1, a_x1T,
         a_x1Ts, a_y, a_yr) = map(sem, (
            "a_h", "a_xc", "a_f", "a_z1", "a_g", "a_z2", "a_t", "a_u", "a_uT", "a_st", "a_mv", "a_ve",
            "a_rs", "a_x1", "a_x1T", "a_x1Ts", "a_y", "a_yr"))
        xt_in, x1_out, x1T_out, y_out = (sems(n, 2) for n in ("xt_in", "x1_out", "x1T_out", "y_out"))
        (b_dm, b_rd, b_q, b_q1, b_q2, b_v, b_g, b_w, b_r, b_rT, b_st, b_mv, b_ve, b_rs, b_n, b_xb,
         b_ng, b_s, b_st2, b_mv2, b_ve2, b_rs2, b_o) = map(sem, (
            "b_dm", "b_rd", "b_q", "b_q1", "b_q2", "b_v", "b_g", "b_w", "b_r", "b_rT", "b_st", "b_mv",
            "b_ve", "b_rs", "b_n", "b_xb", "b_ng", "b_s", "b_st2", "b_mv2", "b_ve2", "b_rs2", "b_o"))
        x1T_in, x1_in, o_out = (sems(n, 2) for n in ("x1T_in", "x1_in", "o_out"))

        block = ctx.enter_context(nc.Block())

        def edge_rows(g):
            if isinstance(g, int) and g >= full:
                return edge[E - GROUP:E, :].rearrange("(p u) d -> p u d", u=TILES)
            return edge[0:full * GROUP, :].rearrange("(g p u) d -> g p u d", p=P, u=TILES)[g]

        def edge_ends(array, g):
            if isinstance(g, int) and g >= full:
                return array[E - GROUP:E].rearrange("(p u) -> p u", u=TILES)
            return array[0:full * GROUP].rearrange("(g p u) -> g p u", p=P, u=TILES)[g]

        def nodes_T(array, n0):
            return array.rearrange("(k p) n -> p k n", p=P)[:, :, bass.ds(n0, CHUNK)]

        def node_rows(array, n0):
            return array[bass.ds(n0, CHUNK), :].rearrange("(b p) d -> p b d", p=P)

        def slot_uses(n, slot, ring):
            return (n - slot + ring - 1) // ring

        def nth_in_slot(n, slot, ring, each):
            return (n - slot) * (each // ring) + each

        def earlier(eng, semaphore, c, ring):
            if not (isinstance(c, int) and c < ring):
                eng.wait_ge(semaphore, c - ring + 1)

        def waits_end(eng):
            eng.sem_inc(waited[eng.engine], 1)

        def last_store_but_one(eng, semaphores, c):
            if isinstance(c, int) and c == C - 1:
                q = (C - 2) % 2
                eng.wait_ge(semaphores[q], 16 * slot_uses(C - 1, q, 2))

        def stored(eng, semaphores, c, m):
            if not (isinstance(c, int) and c < 2):
                eng.wait_ge(semaphores[m % 2], nth_in_slot(c, m % 2, 2, 16) - 16)

        @block.sync
        def _(sp):
            sp.dma_start(src_sb[0][:], edge_ends(src, 0)).then_inc(src_in[0], 16)
            sp.dma_start(win_i[:, 0:full], dst[0:full * GROUP].rearrange("(a g e) -> a g e", a=1, e=GROUP)[:, :, 0],
                         allow_slow_non_contiguous=True
                         ).then_inc(dst_in, 16)
            sp.dma_start(dst_i[:, 0:full, :], dst[0:full * GROUP].rearrange("(g p u) -> p g u", p=P, u=TILES)
                         ).then_inc(dst_in, 16)
            if G > full:
                sp.dma_start(win_i[:, full:G], dst[E - GROUP:E - GROUP + 1].rearrange("(a b) -> a b", a=1)
                             ).then_inc(dst_in, 16)
                sp.dma_start(dst_i[:, full, :], edge_ends(dst, full)).then_inc(dst_in, 16)

            def load_group(first):
                def body(g, slot):
                    sp.wait_ge(e_read, first + g + 1)
                    sp.dma_start(e_sb[slot][:], edge_rows(g)).then_inc(e_in[slot], 16)
                    sp.wait_ge(seg_done, first + g + 1)
                    if not (first == 0 and isinstance(g, int) and g == 0):
                        sp.dma_start(src_sb[slot][:], edge_ends(src, g)).then_inc(src_in[slot], 16)
                return body

            run_groups(sp, load_group(0), 0, RING)
            for tile, array in ((w1T_sb, w1T), (w2T_sb, w2T), (w1m_sb, w1m), (w2m_sb, w2m), (w1u_sb, w1u), (w2u_sb, w2u)):
                sp.dma_start(tile[:], array.rearrange("(k p) m -> p k m", p=P)).then_inc(consts_in, 16)
            sp.dma_start(vt_sb[:], vt).then_inc(consts_in, 16)
            sp.dma_start(vr_sb[:], vr.partition_broadcast(P)).then_inc(consts_in, 16)
            run_groups(sp, load_group(0), RING, G - 1)
            load_group(0)(G - 1, (G - 1) % RING)

            def node_a(s):
                if at := s.at(0):
                    c, n0, m = at
                    earlier(sp, a_h, c, 2)
                    earlier(sp, a_xc, c, 2)
                    waits_end(sp)
                    sp.dma_start(xt_n[m % 2][:], nodes_T(xT, n0)).then_inc(xt_in[m % 2], 16)
                if at := s.at(4):
                    c, n0, m = at
                    sp.wait_ge(a_x1, BLK * (c + 1))
                    last_store_but_one(sp, x1_out, c)
                    waits_end(sp)
                    sp.dma_start(node_rows(x1_dram, n0), x1_n[m % 2][:]).then_inc(x1_out[m % 2], 16)
                if at := s.at(5):
                    c, n0, m = at
                    sp.wait_ge(a_x1Ts, c + 1)
                    last_store_but_one(sp, x1T_out, c)
                    waits_end(sp)
                    sp.dma_start(nodes_T(x1T_dram, n0), x1T_n[m % 2]).then_inc(x1T_out[m % 2], 16)
                if at := s.at(6):
                    c, n0, m = at
                    sp.wait_ge(a_yr, c + 1)
                    last_store_but_one(sp, y_out, c)
                    waits_end(sp)
                    sp.dma_start(node_rows(y_dram, n0), y_n[m % 2]).then_inc(y_out[m % 2], 16)

            run_steps(sp, node_a, C, N, 6)
            run_groups(sp, load_group(G), 0, G - 1)
            load_group(G)(G - 1, (G - 1) % RING)

            for q in range(2):
                sp.wait_ge(x1_out[q], 16 * slot_uses(C, q, 2))
                sp.wait_ge(x1T_out[q], 16 * slot_uses(C, q, 2))

            def node_b(s):
                if at := s.at(0):
                    c, n0, m = at
                    earlier(sp, b_xb, c, 2)
                    waits_end(sp)
                    sp.dma_start(x1_n[m % 2][:], node_rows(x1_dram, n0)).then_inc(x1_in[m % 2], 16)
                if at := s.at(1):
                    c, n0, m = at
                    earlier(sp, b_r, c, 2)
                    waits_end(sp)
                    sp.dma_start(xt_n[m % 2][:], nodes_T(x1T_dram, n0)).then_inc(x1T_in[m % 2], 16)
                if at := s.at(5):
                    c, n0, m = at
                    sp.wait_ge(b_o, BLK * (c + 1))
                    last_store_but_one(sp, o_out, c)
                    waits_end(sp)
                    sp.dma_start(node_rows(out, n0), o_n[m % 2]).then_inc(o_out[m % 2], 16)

            run_steps(sp, node_b, C, N, 5)
            for q in range(2):
                sp.wait_ge(o_out[q], 16 * slot_uses(C, q, 2))
                sp.wait_ge(y_out[q], 16 * slot_uses(C, q, 2))

        @block.gpsimd
        def _(pool):
            def gather(table, first, uses_before):
                def body(g, slot):
                    pool.wait_ge(src_in[slot], nth_in_slot(g, slot, RING, 16) + 16 * uses_before[slot])
                    pool.sem_inc(gather_go, 1)
                    for u in range(TILES):
                        pool.indirect_dma_start(
                            out=m_sb[slot][:, u, :], out_offset=None, in_=table,
                            in_offset=bass.IndirectOffsetOnAxis(ap=src_sb[slot][:, u:u + 1], axis=0),
                        ).then_inc(m_in[slot], 16)
                return body

            pool.iota(iota_i[:], pattern=[[1, WIN]], base=0, channel_multiplier=0).then_inc(consts_made, 1)
            pool.iota(place_i[:], pattern=[[1, TILES]], base=0, channel_multiplier=TILES).then_inc(consts_made, 1)
            pool.memset(root[:], -0.5).then_inc(consts_made, 1)
            pool.memset(eps_t[:], EPS).then_inc(consts_made, 1)
            pool.memset(ident[:], 0.0).then_inc(consts_made, 1)
            pool.wait_ge(consts_made, 5)
            pool.affine_select(out=ident[:], in_=ident[:], compare_op=ALU.not_equal, fill=1.0, base=0,
                               pattern=[[-1, P]], channel_multiplier=1).then_inc(consts_made, 1)
            run_groups(pool, gather(x, 0, [0] * RING), 0, G)

            pool.wait_ge(var_made, 1)
            pool.tensor_tensor(bn_r[:, 0, :], bn_r[:, 0, :], root[:], ALU.pow).then_inc(root_made, 1)
            pool.tensor_tensor(bn_r[:, 1, :], bn_r[:, 1, :], root[:], ALU.pow).then_inc(root_made, 1)

            def rstd(c, m, which, mv_sem, used, ve_sem, rs_sem):
                pool.wait_ge(mv_sem, BLK * (c + 1))
                if not (isinstance(c, int) and c < 2):
                    pool.wait_ge(used, BLK * (c - 1))
                r = rs_n[m % 2][:, which, :]
                pool.tensor_tensor(r, mv_n[m % 2][:, which, :, 1], eps_t[:], ALU.add).then_inc(ve_sem, 1)
                pool.wait_ge(ve_sem, c + 1)
                pool.tensor_tensor(r, r, root[:], ALU.pow).then_inc(rs_sem, 1)

            def node_a(s):
                if at := s.at(4):
                    c, n0, m = at
                    rstd(c, m, 0, a_mv, a_x1, a_ve, a_rs)

            run_steps(pool, node_a, C, N, 4)
            pool.wait_ge(a_h, C)
            pool.memset(acc[:, 0:KD, :], 0.0).then_inc(acc_zero, 1)
            for q in range(2):
                pool.wait_ge(y_out[q], 16 * slot_uses(C, q, 2))
            run_groups(pool, gather(y_dram, G, [slot_uses(G, slot, RING) for slot in range(RING)]), 0, G)

            def node_b(s):
                if at := s.at(5):
                    c, n0, m = at
                    rstd(c, m, 1, b_mv2, b_o, b_ve2, b_rs2)
                if at := s.at(3):
                    c, n0, m = at
                    rstd(c, m, 0, b_mv, b_n, b_ve, b_rs)
                if at := s.at(1):
                    c, n0, m = at
                    if isinstance(c, int) and c == 0:
                        pool.wait_ge(seg_done, 2 * G + RING)
                    pool.wait_ge(x1_in[m % 2], nth_in_slot(c, m % 2, 2, 16))
                    earlier(pool, b_s, c, 4)
                    pool.tensor_tensor(xb_n[m], x1_n[m % 2][:], row("beta"), ALU.add).then_inc(b_xb, 1)
                if at := s.at(4):
                    c, n0, m = at
                    pool.wait_ge(b_n, BLK * (c + 1))
                    pool.tensor_tensor(n_n[m % 2], n_n[m % 2], row("gamma"), ALU.mult).then_inc(b_ng, 1)
                    pool.wait_ge(b_ng, c + 1)
                    pool.tensor_tensor(n_n[m % 2], n_n[m % 2], xb_n[m], ALU.add).then_inc(b_s, 1)

            run_steps(pool, node_b, C, N, 5)

        @block.scalar
        def _(act):
            def relu(g, slot):
                act.wait_ge(added, g + 1)
                act.activation(m_sb[slot], m_sb[slot], ACT.Relu).then_inc(msg_made, 1)

            run_groups(act, relu, 0, G)
            act.wait_ge(bn_made, 1)

            def node_a(s):
                if at := s.at(1):
                    c, n0, m = at
                    act.wait_ge(xt_in[m % 2], nth_in_slot(c, m % 2, 2, 16))
                    earlier(act, a_u, c, 4)
                    if isinstance(c, int) and c == 0:
                        act.wait_ge(seg_done, G + RING)
                    for k in range(KD):
                        last = act.activation(xc_n[m][:, k, :], xt_n[m % 2][:, k, :], ACT.Identity, bias=bn_c[:, 1, k:k + 1])
                    last.then_inc(a_xc, 1)
                    act.wait_ge(a_h, c + 1)
                    earlier(act, a_z1, c, 2)
                    for k in range(KD):
                        last = act.activation(f_n[m % 2][:, k, :], h_n[m][:, k, :], ACT.Identity,
                                              bias=bn_c[:, 0, k:k + 1], scale=bn_s[:, 0, k:k + 1])
                    last.then_inc(a_f, 1)
                if at := s.at(2):
                    c, n0, m = at
                    act.wait_ge(a_z1, c + 1)
                    earlier(act, a_z2, c, 2)
                    for k in range(KD):
                        last = act.activation(g_n[m % 2][:, k, :], bank[2][:, k * CHUNK:(k + 1) * CHUNK], ACT.Gelu,
                                              bias=vec("L0_b1", k))
                    last.then_inc(a_g, 1)
                if at := s.at(5):
                    c, n0, m = at
                    act.wait_ge(a_x1T, c + 1)
                    earlier(act, a_y, c, 2)
                    stored(act, x1T_out, c, m)
                    act.copy(x1T_n[m % 2], bank[5][:].rearrange("p (k n) -> p k n", k=KD)).then_inc(a_x1Ts, 1)

            run_steps(act, node_a, C, N, 5)

            def turn(g, slot, j):
                act.wait_ge(turned, PAIRS * g + j + 1)
                if not (isinstance(g, int) and g < 2):
                    act.wait_ge(z_made, PAIRS * (g - 2) + j + 1)
                act.copy(eT_sb[slot % 2][:, j, :], bank[2 + j][:]).then_inc(eT_made, 1)

            def gelu(g, slot, j):
                act.wait_ge(z_added, PAIRS * g + j + 1)
                v = m_sb[slot][:, 2 * j:2 * j + 2, :]
                act.activation(v, v, ACT.Gelu).then_inc(gelu_made, 1)

            def second_pass(g, slot):
                for j in range(PAIRS):
                    turn(g + 1, slot + 1, j)
                    gelu(g, slot, j)

            for j in range(PAIRS):
                turn(0, 0, j)
            second_pass(0, 0)
            run_groups(act, second_pass, 1, G - 1)
            for j in range(PAIRS):
                gelu(G - 1, (G - 1) % RING, j)

            def node_b(s):
                if at := s.at(1):
                    c, n0, m = at
                    act.wait_ge(b_v, c + 1)
                    earlier(act, b_w, c, 2)
                    for k in range(KH):
                        z = bank[3 + k // KD][:, k % KD * CHUNK:(k % KD + 1) * CHUNK]
                        last = act.activation(g_n[m % 2][:, k, :], z, ACT.Gelu,
                                              bias=vec("b1u_lo" if k < KD else "b1u_hi", k % KD))
                    last.then_inc(b_g, 1)

            run_steps(act, node_b, C, N, 1)

        @block.tensor
        def _(pe):
            def sum_tiles(s, psum, slot, tiles, degrees):
                for u in tiles:
                    for k in range(KD + degrees):
                        values = m_sb[slot][:, u, k * P:(k + 1) * P] if k < KD else ones[:]
                        last = pe.matmul(psum[:, k * WIN:(k + 1) * WIN], values, s[:, u, :],
                                         start=(u == 0 and k == 0), stop=(u == TILES - 1), skip_group_check=True)
                return last

            def sum_all_windows(first, g, slot, degrees):
                pe.sem_inc(gen_go, 1)
                with pe.Fori(0, NW) as k:
                    n = (g + first) * NW + k
                    pe.wait_ge(gen_sel, n + 1)
                    pe.wait_ge(gen_acc, n + 1)
                    sum_tiles(sel[0], bank[0], slot, range(TILES), degrees).then_inc(gen_seg, 1)
                pe.wait_ge(gen_seg, (g + first + 1) * NW)
                pe.sem_inc(seg_done, 1)

            pe.wait_ge(win_ready, 1)
            pe.matmul(bank[7][:, 0:G], ones[0:1, :], win_f[:], start=True, stop=True).then_inc(win_spread, 1)
            pe.wait_ge(extent_ready, 1)
            pe.matmul(bank[6][:, 0:1], ones[:], extent[:, 2:3], start=True, stop=True).then_inc(counted, 1)
            pe.wait_ge(general_made, 1)
            is_general = pe.value_load(general[0:1, 0:1], min_val=0, max_val=1)

            def first_pass(sums):
                def body(g, slot):
                    pe.wait_ge(msg_made, g + 1)
                    sums(g, slot)
                return body

            def first_sums(g, slot):
                pe.wait_ge(sel_made, g + 1)
                pe.wait_ge(acc_done, g + 1)
                sum_tiles(sel[slot % 2], bank[slot % 2], slot, range(TILES), 1).then_inc(seg_done, 1)

            with pe.If(is_general > 0):
                run_groups(pe, first_pass(lambda g, slot: sum_all_windows(0, g, slot, 1)), 0, G)
            with pe.Else():
                run_groups(pe, first_pass(first_sums), 0, G)

            pe.wait_ge(consts_in, 16 * 8)
            pe.wait_ge(consts_made, 6)

            def dense(psum, weights, values, ks, ms, width=CHUNK):
                for i, m in enumerate(ms):
                    for k in ks:
                        last = pe.matmul(psum[:, i * width:(i + 1) * width], weights[:, k, m * P:(m + 1) * P],
                                         values(k), start=(k == 0), stop=(k == len(ks) - 1))
                return last

            def transposes(psum, values, last=None):
                for a in range(2):
                    for b in range(2):
                        last = pe.transpose(psum[:, (2 * b + a) * P:(2 * b + a + 1) * P],
                                            values[:, a, b * P:(b + 1) * P], ident[:])
                return last

            def node_a(s):
                if at := s.at(2):
                    c, n0, m = at
                    pe.wait_ge(a_f, c + 1)
                    earlier(pe, a_g, c, 1)
                    dense(bank[2], w1T_sb, lambda k: f_n[m % 2][:, k, :], range(KD), range(KD)).then_inc(a_z1, 1)
                if at := s.at(3):
                    c, n0, m = at
                    pe.wait_ge(a_g, c + 1)
                    earlier(pe, a_t, c, 1)
                    dense(bank[3], w2T_sb, lambda k: g_n[m % 2][:, k, :], range(KD), range(KD)).then_inc(a_z2, 1)
                if at := s.at(4):
                    c, n0, m = at
                    pe.wait_ge(a_u, c + 1)
                    if not (isinstance(c, int) and c < 1):
                        pe.wait_ge(a_x1, BLK * c)
                    transposes(bank[4], u_n[m % 2]).then_inc(a_uT, 1)
                if at := s.at(5):
                    c, n0, m = at
                    pe.wait_ge(a_x1, BLK * (c + 1))
                    earlier(pe, a_x1Ts, c, 1)
                    transposes(bank[5], x1_n[m % 2]).then_inc(a_x1T, 1)
                if at := s.at(6):
                    c, n0, m = at
                    pe.wait_ge(a_x1Ts, c + 1)
                    earlier(pe, a_yr, c, 1)
                    for b in range(BLK):
                        for k in range(KD):
                            last = pe.matmul(bank[6][:, b * D:(b + 1) * D], x1T_n[m % 2][:, k, b * P:(b + 1) * P],
                                             w1m_sb[:, k, :], start=(k == 0), stop=(k == KD - 1))
                    last.then_inc(a_y, 1)

            run_steps(pe, node_a, C, N, 6)
            pe.wait_ge(a_yr, C)

            def turn(g, slot, j):
                if j == 0:
                    pe.wait_ge(e_in[slot % RING],
                               nth_in_slot(g, slot % RING, RING, 16) + 16 * slot_uses(G, slot % RING, RING))
                if not (isinstance(g, int) and g < 1):
                    pe.wait_ge(eT_made, PAIRS * (g - 1) + j + 1)
                for t in range(2):
                    for k in range(KD):
                        last = pe.transpose(bank[2 + j][:, (t * KD + k) * P:(t * KD + k + 1) * P],
                                            e_sb[slot % RING][:, 2 * j + t, k * P:(k + 1) * P], ident[:])
                last.then_inc(turned, 1)
                if j == PAIRS - 1:
                    pe.wait_ge(turned, PAIRS * (g + 1))
                    pe.sem_inc(e_read, 1)

            def product(g, slot, j):
                pe.wait_ge(eT_made, PAIRS * g + j + 1)
                if not (isinstance(g, int) and g < 1):
                    pe.wait_ge(z_added, PAIRS * (g - 1) + j + 1)
                for t in range(2):
                    for k in range(KD):
                        last = pe.matmul(bank[5 + j][:, t * D:(t + 1) * D],
                                         eT_sb[slot % 2][:, j, (t * KD + k) * P:(t * KD + k + 1) * P],
                                         w1m_sb[:, k, :], start=(k == 0), stop=(k == KD - 1))
                last.then_inc(z_made, 1)

            def second_sums(g, slot, j):
                pe.wait_ge(gelu_made, PAIRS * g + j + 1)
                if j == 0:
                    pe.wait_ge(sel_made, G + g + 1)
                    pe.wait_ge(acc_done, G + g + 1)
                last = sum_tiles(sel[slot % 2], bank[slot % 2], slot % RING, range(2 * j, 2 * j + 2), 0)
                if j == PAIRS - 1:
                    last.then_inc(seg_done, 1)

            def second_pass(g, slot):
                for j in range(PAIRS):
                    turn(g + 1, slot + 1, j)
                    product(g, slot, j)
                    second_sums(g - 1, slot - 1, j)

            def second_pass_general(g, slot):
                for j in range(PAIRS):
                    turn(g + 1, slot + 1, j)
                    product(g, slot, j)
                pe.wait_ge(gelu_made, PAIRS * g)
                sum_all_windows(G, g - 1, (slot - 1) % RING, 0)

            for j in range(PAIRS):
                turn(0, 0, j)
            for j in range(PAIRS):
                turn(1, 1, j)
                product(0, 0, j)
            with pe.If(is_general > 0):
                run_groups(pe, second_pass_general, 1, G - 1)
                for j in range(PAIRS):
                    product(G - 1, (G - 1) % RING, j)
                pe.wait_ge(gelu_made, PAIRS * (G - 1))
                sum_all_windows(G, G - 2, (G - 2) % RING, 0)
                pe.wait_ge(gelu_made, PAIRS * G)
                sum_all_windows(G, G - 1, (G - 1) % RING, 0)
            with pe.Else():
                run_groups(pe, second_pass, 1, G - 1)
                for j in range(PAIRS):
                    product(G - 1, (G - 1) % RING, j)
                    second_sums(G - 2, (G - 2) % RING, j)
                for j in range(PAIRS):
                    second_sums(G - 1, (G - 1) % RING, j)

            pe.wait_ge(acc_done, 2 * G + 2)

            def node_b(s):
                if at := s.at(0):
                    c, n0, m = at
                    if not (isinstance(c, int) and c < 1):
                        pe.wait_ge(b_q1, KD * c)
                    dense(bank[2], w2m_sb, lambda k: acc[:, k, bass.ds(n0, CHUNK)], range(KD), range(KD)).then_inc(b_q, 1)
                if at := s.at(1):
                    c, n0, m = at
                    pe.wait_ge(b_q2, c + 1)
                    earlier(pe, b_g, c, 1)
                    dense(bank[3], w1u_sb, lambda k: q_n[m % 2][:, k, :], range(KD), range(0, KD))
                    dense(bank[4], w1u_sb, lambda k: q_n[m % 2][:, k, :], range(KD), range(KD, KH)).then_inc(b_v, 1)
                if at := s.at(2):
                    c, n0, m = at
                    pe.wait_ge(b_g, c + 1)
                    earlier(pe, b_r, c, 1)
                    dense(bank[5], w2u_sb, lambda k: g_n[m % 2][:, k, :], range(KH), range(KD)).then_inc(b_w, 1)
                if at := s.at(3):
                    c, n0, m = at
                    pe.wait_ge(b_r, c + 1)
                    if not (isinstance(c, int) and c < 1):
                        pe.wait_ge(b_n, BLK * c)
                    transposes(bank[6], r_n[m % 2]).then_inc(b_rT, 1)

            run_steps(pe, node_b, C, N, 3)

        @block.vector
        def _(dve):
            steps = [0]

            def link(instruction):
                steps[0] += 1
                instruction.then_inc(prep, 1)
                dve.wait_ge(prep, steps[0])

            dve.sem_inc(e_read, RING)
            dve.sem_inc(seg_done, RING)
            dve.sem_inc(acc_done, 2)
            dve.sem_inc(gen_acc, 1)
            link(dve.memset(ones[:], 1.0))
            dve.wait_ge(dst_in, 16 * (4 if G > full else 2))
            dve.tensor_copy(win_f[:], win_i[:]).then_inc(win_ready, 1)
            link(dve.tensor_copy(dst_f[:], dst_i[:]))
            dve.wait_ge(consts_made, 4)
            link(dve.tensor_copy(iota[:], iota_i[:]))
            if repeated:
                link(dve.tensor_scalar(repeat[:], place_i[:], float(repeated), OUTSIDE, ALU.is_lt, ALU.mult))
            dve.wait_ge(win_spread, 1)
            link(dve.tensor_copy(win_bc[:], bank[7][:, 0:G]))
            link(dve.tensor_tensor(rel[:], dst_f[:], win_bc[:].unsqueeze(2).broadcast_to([P, G, TILES]), ALU.subtract))
            dve.tensor_reduce(extent[:, 0:1], rel[:].rearrange("p g u -> p (g u)"), AX_X, ALU.min)
            link(dve.tensor_reduce(extent[:, 1:2], rel[:].rearrange("p g u -> p (g u)"), AX_X, ALU.max))
            link(dve.tensor_scalar(extent[:, 3:4], extent[:, 1:2], float(WIN - 1), None, ALU.is_gt))
            link(dve.tensor_scalar(extent[:, 0:1], extent[:, 0:1], 0.0, None, ALU.is_lt))
            dve.tensor_tensor(extent[:, 2:3], extent[:, 0:1], extent[:, 3:4], ALU.max).then_inc(extent_ready, 1)
            dve.wait_ge(counted, 1)
            dve.tensor_scalar(general[:], bank[6][:, 0:1], 1.0, None, ALU.min).then_inc(general_made, 1)
            if repeated:
                link(dve.tensor_tensor(rel[:, G - 1, :], rel[:, G - 1, :], repeat[:], ALU.add))
                link(dve.tensor_tensor(dst_f[:, G - 1, :], dst_f[:, G - 1, :], repeat[:], ALU.add))
            dve.memset(acc[:], 0.0).then_inc(acc_zero, 1)
            dve.wait_ge(general_made, 1)
            is_general = dve.value_load(general[0:1, 0:1], min_val=0, max_val=1)

            def select(s, positions):
                return dve.tensor_tensor(s[:], iota[:].unsqueeze(1).broadcast_to([P, TILES, WIN]),
                                         positions.unsqueeze(2).broadcast_to([P, TILES, WIN]), ALU.is_equal)

            def selection(first, g, slot):
                dve.wait_ge(seg_done, first + g + RING - 1)
                select(sel[slot % 2], rel[:, bass.ds(g, 1), :].rearrange("p a u -> p (a u)")
                       ).then_inc(sel_made, 1)

            def accumulate(first, g, slot, rows):
                w = dve.value_load(win_i[0:1, bass.ds(g, 1)], min_val=0, max_val=N - 1)
                dve.wait_ge(seg_done, first + g + 1 + RING)
                dve.wait_ge(acc_done, first + g + 2)
                at_w = acc[:, 0:rows, bass.ds(w, WIN)]
                dve.tensor_tensor(at_w, at_w, bank[slot % 2][:, 0:rows * WIN].rearrange("p (k n) -> p k n", n=WIN),
                                  ALU.add).then_inc(acc_done, 1)

            def all_windows(first, g, rows):
                made = (g + first) * (NW + 1)
                dve.wait_ge(acc_done, first + g + 2)
                dve.tensor_copy(rel_k[:], dst_f[:, bass.ds(g, 1), :].rearrange("p a u -> p (a u)")).then_inc(gen_rel, 1)
                with dve.Fori(0, NW) as k:
                    n = (g + first) * NW + k
                    dve.wait_ge(gen_rel, made + k + 1)
                    select(sel[0], rel_k[:]).then_inc(gen_sel, 1)
                    dve.wait_ge(gen_sel, n + 1)
                    dve.tensor_scalar(rel_k[:], rel_k[:], float(-WIN), None, ALU.add).then_inc(gen_rel, 1)
                    dve.wait_ge(gen_seg, n + 1)
                    at_w = acc[:, 0:rows, bass.ds(k * WIN, WIN)]
                    dve.tensor_tensor(at_w, at_w, bank[0][:, 0:rows * WIN].rearrange("p (k n) -> p k n", n=WIN),
                                      ALU.add).then_inc(gen_acc, 1)
                dve.wait_ge(gen_acc, (g + first + 1) * NW + 1)
                dve.sem_inc(acc_done, 1)

            def add_edges(g, slot):
                dve.wait_ge(e_in[slot], nth_in_slot(g, slot, RING, 16))
                dve.wait_ge(m_in[slot], nth_in_slot(g, slot, RING, 16 * TILES))
                dve.tensor_tensor(m_sb[slot], m_sb[slot], e_sb[slot][:], ALU.add).then_inc(added, 1)
                dve.wait_ge(added, g + 1)
                dve.sem_inc(e_read, 1)

            def first_pass(g, slot):
                selection(0, g, slot)
                add_edges(g, slot)
                accumulate(0, g - 1, (slot - 1) % RING, KD + 1)

            def first_pass_general(g, slot):
                add_edges(g, slot)
                all_windows(0, g, KD + 1)

            dve.wait_ge(acc_zero, 1)
            with dve.If(is_general > 0):
                run_groups(dve, first_pass_general, 0, G)
            with dve.Else():
                selection(0, 0, 0)
                add_edges(0, 0)
                run_groups(dve, first_pass, 1, G)
                accumulate(0, G - 1, (G - 1) % RING, KD + 1)

            dve.wait_ge(consts_in, 16 * 8)
            v = {name: vt_sb[:, VT.index(name), :] for name in VT}
            dve.tensor_scalar(bn_r[:, 0, :], v["bn1_var"], EPS, None, ALU.add)
            dve.tensor_scalar(bn_r[:, 1, :], v["bn2_var"], EPS, None, ALU.add).then_inc(var_made, 1)
            dve.wait_ge(root_made, 2)
            link(dve.tensor_tensor(bn_s[:, 0, :], bn_r[:, 0, :], v["bn1_gamma"], ALU.mult))
            link(dve.tensor_tensor(bn_s[:, 1, :], bn_r[:, 1, :], v["bn2_gamma"], ALU.mult))
            link(dve.tensor_tensor(bn_t[:, 0, :], bn_s[:, 0, :], v["bn1_mean"], ALU.mult))
            link(dve.tensor_tensor(bn_c[:, 0, :], v["bn1_beta"], bn_t[:, 0, :], ALU.subtract))
            link(dve.tensor_tensor(bn_t[:, 1, :], v["L0_b2"], v["bn2_mean"], ALU.subtract))
            link(dve.tensor_tensor(bn_t[:, 1, :], bn_t[:, 1, :], bn_s[:, 1, :], ALU.mult))
            dve.tensor_tensor(bn_c[:, 1, :], bn_t[:, 1, :], v["bn2_beta"], ALU.add).then_inc(bn_made, 1)
            dve.wait_ge(bn_made, 1)
            dve.wait_ge(acc_done, G + 2)

            def statistics(m, which, values, c, st_sem, mv_sem, ve_sem):
                for b in range(BLK):
                    dve.bn_stats(st_n[m % 2][:, which, b, :], values(b)).then_inc(st_sem, 1)
                if not (isinstance(c, int) and c < 2):
                    dve.wait_ge(ve_sem, c - 1)
                dve.wait_ge(st_sem, BLK * (c + 1))
                waits_end(dve)
                for b in range(BLK):
                    dve.bn_aggr(mv_n[m % 2][:, which, b, :], st_n[m % 2][:, which, b, :]).then_inc(mv_sem, 1)

            def norm(m, which, to, values, c, mv_sem, rs_sem, done):
                dve.wait_ge(mv_sem, BLK * (c + 1))
                dve.wait_ge(rs_sem, c + 1)
                for b in range(BLK):
                    dve.tensor_scalar(to[:, b, :], values(b), mv_n[m % 2][:, which, b, 0:1],
                                      rs_n[m % 2][:, which, b:b + 1], ALU.subtract, ALU.mult).then_inc(done, 1)

            def node_a(s):
                if at := s.at(1):
                    c, n0, m = at
                    dve.wait_ge(xt_in[m % 2], nth_in_slot(c, m % 2, 2, 16))
                    earlier(dve, a_f, c, 4)
                    dve.scalar_tensor_tensor(out=h_n[m], in0=xt_n[m % 2][:], scalar=2.0,
                                             in1=acc[:, 0:KD, bass.ds(n0, CHUNK)], op0=ALU.mult, op1=ALU.add
                                             ).then_inc(a_h, 1)
                if at := s.at(3):
                    c, n0, m = at
                    dve.wait_ge(a_z2, c + 1)
                    dve.wait_ge(a_h, c + 1)
                    dve.tensor_tensor(h_n[m], bank[3][:].rearrange("p (k n) -> p k n", k=KD), h_n[m], ALU.add
                                      ).then_inc(a_t, 1)
                if at := s.at(4):
                    c, n0, m = at
                    dve.wait_ge(a_uT, c + 1)
                    statistics(m, 0, lambda b: bank[4][:, b * D:(b + 1) * D], c, a_st, a_mv, a_ve)
                if at := s.at(3):
                    c, n0, m = at
                    dve.wait_ge(a_t, c + 1)
                    dve.wait_ge(a_xc, c + 1)
                    earlier(dve, a_uT, c, 2)
                    for k in range(KD):
                        last = dve.scalar_tensor_tensor(out=u_n[m % 2][:, k, :], in0=h_n[m][:, k, :],
                                                        scalar=bn_s[:, 1, k:k + 1], in1=xc_n[m][:, k, :],
                                                        op0=ALU.mult, op1=ALU.add)
                    last.then_inc(a_u, 1)
                if at := s.at(6):
                    c, n0, m = at
                    dve.wait_ge(a_y, c + 1)
                    stored(dve, y_out, c, m)
                    dve.tensor_tensor(y_n[m % 2], bank[6][:].rearrange("p (b d) -> p b d", d=D), row("b1m"), ALU.add
                                      ).then_inc(a_yr, 1)
                if at := s.at(4):
                    c, n0, m = at
                    stored(dve, x1_out, c, m)
                    earlier(dve, a_x1T, c, 2)
                    norm(m, 0, x1_n[m % 2], lambda b: bank[4][:, b * D:(b + 1) * D], c, a_mv, a_rs, a_x1)

            run_steps(dve, node_a, C, N, 6)
            dve.wait_ge(acc_zero, 2)

            def add_rows(g, slot, j):
                if j == 0:
                    dve.wait_ge(m_in[slot], nth_in_slot(g, slot, RING, 16 * TILES)
                                + 16 * TILES * slot_uses(G, slot, RING))
                dve.wait_ge(z_made, PAIRS * g + j + 1)
                v2 = m_sb[slot][:, 2 * j:2 * j + 2, :]
                dve.tensor_tensor(v2, bank[5 + j][:].rearrange("p (t d) -> p t d", d=D), v2, ALU.add
                                  ).then_inc(z_added, 1)

            def second_pass(g, slot):
                selection(G, g, slot)
                add_rows(g, slot, 0)
                add_rows(g, slot, 1)
                accumulate(G, g - 1, (slot - 1) % RING, KD)
                add_rows(g, slot, 2)

            def second_pass_general(g, slot):
                for j in range(PAIRS):
                    add_rows(g, slot, j)
                all_windows(G, g - 1, KD)

            with dve.If(is_general > 0):
                for j in range(PAIRS):
                    add_rows(0, 0, j)
                run_groups(dve, second_pass_general, 1, G)
                all_windows(G, G - 1, KD)
            with dve.Else():
                selection(G, 0, 0)
                for j in range(PAIRS):
                    add_rows(0, 0, j)
                run_groups(dve, second_pass, 1, G)
                accumulate(G, G - 1, (G - 1) % RING, KD)
            dve.wait_ge(acc_done, 2 * G + 2)

            def node_b(s):
                if at := s.at(5):
                    c, n0, m = at
                    dve.wait_ge(b_s, c + 1)
                    statistics(m, 1, lambda b: n_n[m % 2][:, b, :], c, b_st2, b_mv2, b_ve2)
                if at := s.at(0):
                    c, n0, m = at
                    degree = acc[:, KD, bass.ds(n0, CHUNK)]
                    dve.tensor_scalar(f_n[m % 2][:, 0, :], degree, 1.0, None, ALU.max).then_inc(b_dm, 1)
                    dve.wait_ge(b_dm, c + 1)
                    dve.reciprocal(f_n[m % 2][:, 1, :], f_n[m % 2][:, 0, :]).then_inc(b_rd, 1)
                if at := s.at(5):
                    c, n0, m = at
                    stored(dve, o_out, c, m)
                    norm(m, 1, o_n[m % 2], lambda b: n_n[m % 2][:, b, :], c, b_mv2, b_rs2, b_o)
                if at := s.at(3):
                    c, n0, m = at
                    dve.wait_ge(b_rT, c + 1)
                    statistics(m, 0, lambda b: bank[6][:, b * D:(b + 1) * D], c, b_st, b_mv, b_ve)
                if at := s.at(0):
                    c, n0, m = at
                    degree = acc[:, KD, bass.ds(n0, CHUNK)]
                    dve.wait_ge(b_q, c + 1)
                    earlier(dve, b_v, c, 2)
                    for k in range(KD):
                        dve.scalar_tensor_tensor(out=q_n[m % 2][:, k, :], in0=degree, scalar=vec("b2m", k),
                                                 in1=bank[2][:, k * CHUNK:(k + 1) * CHUNK], op0=ALU.mult, op1=ALU.add
                                                 ).then_inc(b_q1, 1)
                if at := s.at(2):
                    c, n0, m = at
                    dve.wait_ge(b_w, c + 1)
                    dve.wait_ge(x1T_in[m % 2], nth_in_slot(c, m % 2, 2, 16))
                    earlier(dve, b_rT, c, 2)
                    for k in range(KD):
                        last = dve.scalar_tensor_tensor(out=r_n[m % 2][:, k, :], in0=bank[5][:, k * CHUNK:(k + 1) * CHUNK],
                                                        scalar=vec("b2u", k), in1=xt_n[m % 2][:, k, :],
                                                        op0=ALU.add, op1=ALU.add)
                    last.then_inc(b_r, 1)
                if at := s.at(0):
                    c, n0, m = at
                    dve.wait_ge(b_q1, KD * (c + 1))
                    dve.wait_ge(b_rd, c + 1)
                    dve.tensor_tensor(q_n[m % 2], q_n[m % 2],
                                      f_n[m % 2][:, 1:2, :].broadcast_to([P, KD, CHUNK]), ALU.mult).then_inc(b_q2, 1)
                if at := s.at(3):
                    c, n0, m = at
                    norm(m, 0, n_n[m % 2], lambda b: bank[6][:, b * D:(b + 1) * D], c, b_mv, b_rs, b_n)

            run_steps(dve, node_b, C, N, 5)


def kernel(**inputs):
    import concourse.bacc as bacc
    from concourse.bass_utils import run_bass_kernel_spmd

    a = {k: np.asarray(v) for k, v in inputs.items()}
    names = {"L0_b1": "L0_gnn_b1", "L0_b2": "L0_gnn_b2", "b2m": "L1_gnn_b2m", "b2u": "L1_gnn_b2u"}
    per_feature = [a[names.get(n, "L0_gnn_" + n)] for n in VT[:-2]]
    per_feature += [a["L1_gnn_b1u"][0:D], a["L1_gnn_b1u"][D:2 * D]]
    arrays = {
        "x": a["x"], "xT": a["x"].T, "src": a["src"], "dst": a["dst"], "edge": a["edge_attr_256"],
        "w1T": a["L0_gnn_W1"].T, "w2T": a["L0_gnn_W2"].T, "w1m": a["L1_gnn_W1m"], "w2m": a["L1_gnn_W2m"],
        "w1u": a["L1_gnn_W1u"], "w2u": a["L1_gnn_W2u"],
        "vt": np.stack(per_feature).reshape(len(VT), KD, P).transpose(2, 0, 1),
        "vr": np.stack([a["L1_gnn_b1m"], a["L1_gnn_gamma"], a["L1_gnn_beta"]]),
    }
    arrays = {k: np.ascontiguousarray(v) for k, v in arrays.items()}
    nc = bacc.Bacc("TRN2", target_bir_lowering=False, num_devices=1)
    args = {k: nc.dram_tensor(f"in_{k}", v.shape, mybir.dt.from_np(v.dtype), kind="ExternalInput").ap()
            for k, v in arrays.items()}
    out = nc.dram_tensor("out", list(a["x"].shape), F32, kind="ExternalOutput").ap()
    build(nc, *args.values(), out)
    result = run_bass_kernel_spmd(nc, [{f"in_{k}": v for k, v in arrays.items()}], core_ids=[0])
    return result.results[0]["out"]
```

```python
from contextlib import ExitStack

import numpy as np

import concourse.bass as bass
from concourse import mybir

ALU = mybir.AluOpType
ACT = mybir.ActivationFunctionType
AX_X = mybir.AxisListType.X
F32 = mybir.dt.float32
F32R = mybir.dt.float32r
BF16 = mybir.dt.bfloat16
I32 = mybir.dt.int32

P = 128
D = 256
KD = D // P
TILES = 6
PAIRS = TILES // 2
GROUP = TILES * P
WIN = 64
RING = 4
CHUNK = 256
BLK = CHUNK // P
STEPS = 4
EPS = 1e-5
OUTSIDE = -1.0e6

VT = ["L0_b1", "L0_b2", "bn1_gamma", "bn1_beta", "bn1_mean", "bn1_var",
      "bn2_gamma", "bn2_beta", "bn2_mean", "bn2_var", "b2m", "b2u", "b1u_lo", "b1u_hi"]
VR = ["b1m", "gamma", "beta"]


class Step:

    def __init__(self, i, phase, chunks, nodes):
        self.i, self.phase, self.chunks, self.nodes = i, phase, chunks, nodes

    def at(self, offset):
        c = self.i - offset
        if isinstance(self.i, int):
            if not 0 <= c < self.chunks:
                return None
            return c, min(c * CHUNK, self.nodes - CHUNK), c % STEPS
        return c, c * CHUNK, (self.phase - offset) % STEPS


def run_steps(eng, body, chunks, nodes, depth):
    first = 2 * STEPS
    rounds = max(0, (chunks - 1 - first) // STEPS)
    for i in range(min(first, chunks + depth)):
        body(Step(i, i % STEPS, chunks, nodes))
    if rounds:
        with eng.Fori(0, rounds) as r:
            for s in range(STEPS):
                body(Step(r * STEPS + (first + s), s, chunks, nodes))
    for i in range(first + rounds * STEPS, chunks + depth):
        body(Step(i, i % STEPS, chunks, nodes))


def run_groups(eng, body, start, stop, ring=RING):
    rounds = (stop - start) // ring
    if rounds:
        with eng.Fori(0, rounds) as r:
            for s in range(ring):
                body(r * ring + (start + s), (start + s) % ring)
    for g in range(start + rounds * ring, stop):
        body(g, g % ring)


def build(nc, x, xT, src, dst, edge, edgeT, w1T, w2T, w1m, w2m, w1u, w2u, vt, vr, out):
    N = x.shape[0]
    E = edge.shape[0]
    full = E // GROUP
    G = -(-E // GROUP)
    repeated = G * GROUP - E
    NW = -(-N // WIN)
    NPAD = N + WIN
    C = -(-N // CHUNK)
    H2 = w1u.shape[1]
    KH = H2 // P
    DEG = D + KD * WIN
    assert 2 * RING < full and G <= 512 and C >= 2 and KH == 2 * KD

    y_dram = nc.dram_tensor("y_scratch", [N, D], F32, kind="Internal").ap()
    x1_dram = nc.dram_tensor("x1_scratch", [N, D], F32, kind="Internal").ap()
    x1T_dram = nc.dram_tensor("x1T_scratch", [D, N], F32, kind="Internal").ap()

    with ExitStack() as ctx:
        def sb(name, shape, dt=F32):
            return ctx.enter_context(nc.sbuf_tensor(name, shape, dt))

        def sem(name):
            return ctx.enter_context(nc.semaphore(name))

        def sems(name, n):
            return [sem(f"{name}{i}") for i in range(n)]

        bank = [ctx.enter_context(nc.psum_tensor(f"bank{i}", [P, 512], F32)) for i in range(8)]

        acc = sb("acc", [P, KD + 1, NPAD])
        e_all = sb("e_all", [P, RING * TILES * D])
        e_sb = [e_all[:, s * TILES * D:(s + 1) * TILES * D].rearrange("p (u d) -> p u d", d=D)
                for s in range(RING)]
        eT_sb = [e_all[:, s * TILES * D:(s + 1) * TILES * D].rearrange("p (k e) -> p k e", k=KD)
                 for s in range(RING)]
        m_all = sb("m_all", [P, RING * TILES * D])
        m_sb = [m_all[:, s * TILES * D:(s + 1) * TILES * D].rearrange("p (u d) -> p u d", d=D)
                for s in range(RING)]
        src_sb = [sb(f"src{s}", [P, TILES], I32) for s in range(2 * RING)]
        eT_hi, eT_lo, m_hi, m_lo = ([sb(f"{n}{j}", [P, 2 * D], F32R) for j in range(PAIRS)]
                                    for n in ("eT_hi", "eT_lo", "m_hi", "m_lo"))
        sel = [sb(f"sel{s}", [P, TILES, P], F32R) for s in range(2)]
        sel_b = [sb(f"sel_b{s}", [P, TILES, WIN], BF16) for s in range(2)]
        sum_n = [sb(f"sum_n{s}", [WIN, D]) for s in range(2)]
        dst_i = acc[:, 0, 0:G * TILES].rearrange("p (g u) -> p g u", u=TILES).bitcast(I32)
        dst_f = sb("dst_f", [P, G, TILES])
        rel = sb("rel", [P, G, TILES])
        win_i = sb("win_i", [1, G], I32)
        win_f = sb("win_f", [1, G])
        win_bc = sb("win_bc", [P, G])
        iota_i = sb("iota_i", [P, WIN], I32)
        iota = sb("iota", [P, WIN])
        place_i = sb("place_i", [P, TILES], I32)
        repeat = sb("repeat", [P, TILES])
        extent = sb("extent", [P, 4])
        general = sb("general", [P, 1], I32)
        rel_k = sb("rel_k", [P, TILES])
        ones = sb("ones", [P, P])
        ones_b = sb("ones_b", [P, P], BF16)
        ident = sb("ident", [P, P])
        root = sb("root", [P, BLK])
        eps_t = sb("eps_t", [P, BLK])
        w1T_sb = sb("w1T_sb", [P, KD, D])
        w2T_sb = sb("w2T_sb", [P, KD, D])
        w1m_sb = sb("w1m_sb", [P, KD, D])
        w1m_hi = sb("w1m_hi", [P, KD, D], F32R)
        w1m_lo = sb("w1m_lo", [P, KD, D], F32R)
        w2m_sb = sb("w2m_sb", [P, KD, D])
        w1u_sb = sb("w1u_sb", [P, KD, H2])
        w2u_sb = sb("w2u_sb", [P, KH, D])
        vt_sb = sb("vt_sb", [P, len(VT), KD])
        vr_sb = sb("vr_sb", [P, len(VR), D])
        bn_r = sb("bn_r", [P, 2, KD])
        bn_s = sb("bn_s", [P, 2, KD])
        bn_c = sb("bn_c", [P, 2, KD])
        bn_t = sb("bn_t", [P, 2, KD])

        def vec(name, k):
            return vt_sb[:, VT.index(name), k:k + 1]

        def row(name):
            return vr_sb[:, VR.index(name), :].unsqueeze(1).broadcast_to([P, BLK, D])

        UNIT = KD * CHUNK

        def spare(first, n, inner=CHUNK, of=m_all, units=1):
            return [of[:, (first + i * units) * UNIT:(first + (i + 1) * units) * UNIT]
                    .rearrange("p (k n) -> p k n", n=inner) for i in range(n)]

        h_n = spare(0, 4)
        xc_n = spare(4, 4)
        u_n = spare(8, 2)
        y_n = spare(10, 2, D)
        q_n = spare(0, 2)
        r_n = spare(2, 2)
        xb_n = spare(4, 4, D)
        n_n = spare(8, 2, D)
        o_n = spare(10, 2, D)
        xt_n = spare(0, 2, of=e_all)
        f_n = spare(2, 2, of=e_all)
        x1_n = spare(4, 2, D, of=e_all)
        g_n = spare(6, 2, of=e_all, units=KH // KD)
        x1T_n = [g_n[i][:, KD:KH, :] for i in range(2)]
        st_n = [sb(f"st_n{i}", [P, 2, BLK, 6]) for i in range(2)]
        mv_n = [sb(f"mv_n{i}", [P, 2, BLK, 2]) for i in range(2)]
        rs_n = [sb(f"rs_n{i}", [P, 2, BLK]) for i in range(2)]

        dst_in = sem("dst_in")
        consts_in = sem("consts_in")
        consts_made = sem("consts_made")
        prep = sem("prep")
        win_ready = sem("win_ready")
        win_spread = sem("win_spread")
        extent_ready = sem("extent_ready")
        counted = sem("counted")
        general_made = sem("general_made")
        var_made = sem("var_made")
        root_made = sem("root_made")
        bn_made = sem("bn_made")
        e_in = sems("e_in", RING)
        src_in = sems("src_in", 2 * RING)
        m_in = sems("m_in", RING)
        gather_go = sem("gather_go")
        sel_made = sem("sel_made")
        sum_copied = sem("sum_copied")
        sum_turned = sem("sum_turned")
        acc_done = sem("acc_done")
        gen_go = sem("gen_go")
        gen_rel = sem("gen_rel")
        gen_sel = sem("gen_sel")
        gen_seg = sem("gen_seg")
        gen_copied = sem("gen_copied")
        gen_turned = sem("gen_turned")
        gen_acc = sem("gen_acc")
        eT_high = sem("eT_high")
        eT_low = sem("eT_low")
        z_made = sem("z_made")
        added = sem("added")
        act_high = sem("act_high")
        act_made = sem("act_made")
        act_low = sem("act_low")
        pair_summed = sem("pair_summed")
        waited = {e: sem(f"waited_{e.name}") for e in (nc.sync.engine, nc.vector.engine, nc.tensor.engine)}
        w_split = sem("w_split")
        acc_zero = sem("acc_zero")

        (a_h, a_xc, a_f, a_z1, a_g, a_z2, a_t, a_u, a_uT, a_st, a_mv, a_ve, a_rs, a_x1, a_x1T,
         a_x1Ts, a_y, a_yr) = map(sem, (
            "a_h", "a_xc", "a_f", "a_z1", "a_g", "a_z2", "a_t", "a_u", "a_uT", "a_st", "a_mv", "a_ve",
            "a_rs", "a_x1", "a_x1T", "a_x1Ts", "a_y", "a_yr"))
        xt_in, x1_out, x1T_out, y_out = (sems(n, 2) for n in ("xt_in", "x1_out", "x1T_out", "y_out"))
        (b_dm, b_rd, b_q, b_q1, b_q2, b_v, b_g, b_w, b_r, b_rT, b_st, b_mv, b_ve, b_rs, b_n, b_xb,
         b_ng, b_s, b_st2, b_mv2, b_ve2, b_rs2, b_o) = map(sem, (
            "b_dm", "b_rd", "b_q", "b_q1", "b_q2", "b_v", "b_g", "b_w", "b_r", "b_rT", "b_st", "b_mv",
            "b_ve", "b_rs", "b_n", "b_xb", "b_ng", "b_s", "b_st2", "b_mv2", "b_ve2", "b_rs2", "b_o"))
        x1T_in, x1_in, o_out = (sems(n, 2) for n in ("x1T_in", "x1_in", "o_out"))

        block = ctx.enter_context(nc.Block())

        def edge_rows(g):
            if isinstance(g, int) and g >= full:
                return edge[E - GROUP:E, :].rearrange("(p u) d -> p u d", u=TILES)
            return edge[0:full * GROUP, :].rearrange("(g p u) d -> g p u d", p=P, u=TILES)[g]

        def edge_columns(g):
            if isinstance(g, int) and g >= full:
                return edgeT[:, E - GROUP:E].rearrange("(k p) e -> p k e", p=P)
            return edgeT[:, 0:full * GROUP].rearrange("(k p) (g e) -> g p k e", p=P, e=GROUP)[g]

        def pair_of(eT, j):
            return eT.rearrange("p k (e u) -> p k u e", u=TILES)[:, :, 2 * j:2 * j + 2, :]

        def edge_ends(array, g):
            if isinstance(g, int) and g >= full:
                return array[E - GROUP:E].rearrange("(p u) -> p u", u=TILES)
            return array[0:full * GROUP].rearrange("(g p u) -> g p u", p=P, u=TILES)[g]

        def z_bank(slot, j):
            return bank[2 + slot % 2 * PAIRS + j]

        def nodes_T(array, n0):
            return array.rearrange("(k p) n -> p k n", p=P)[:, :, bass.ds(n0, CHUNK)]

        def node_rows(array, n0):
            return array[bass.ds(n0, CHUNK), :].rearrange("(b p) d -> p b d", p=P)

        def slot_uses(n, slot, ring):
            return (n - slot + ring - 1) // ring

        def nth_in_slot(n, slot, ring, each):
            return (n - slot) * (each // ring) + each

        def earlier(eng, semaphore, c, ring):
            if not (isinstance(c, int) and c < ring):
                eng.wait_ge(semaphore, c - ring + 1)

        def waits_end(eng):
            eng.sem_inc(waited[eng.engine], 1)

        def last_store_but_one(eng, semaphores, c):
            if isinstance(c, int) and c == C - 1:
                q = (C - 2) % 2
                eng.wait_ge(semaphores[q], 16 * slot_uses(C - 1, q, 2))

        def stored(eng, semaphores, c, m):
            if not (isinstance(c, int) and c < 2):
                eng.wait_ge(semaphores[m % 2], nth_in_slot(c, m % 2, 2, 16) - 16)

        @block.sync
        def _(sp):
            sp.dma_start(src_sb[0][:], edge_ends(src, 0)).then_inc(src_in[0], 16)
            sp.dma_start(win_i[:, 0:full], dst[0:full * GROUP].rearrange("(a g e) -> a g e", a=1, e=GROUP)[:, :, 0],
                         allow_slow_non_contiguous=True
                         ).then_inc(dst_in, 16)
            sp.dma_start(dst_i[:, 0:full, :], dst[0:full * GROUP].rearrange("(g p u) -> p g u", p=P, u=TILES)
                         ).then_inc(dst_in, 16)
            if G > full:
                sp.dma_start(win_i[:, full:G], dst[E - GROUP:E - GROUP + 1].rearrange("(a b) -> a b", a=1)
                             ).then_inc(dst_in, 16)
                sp.dma_start(dst_i[:, full, :], edge_ends(dst, full)).then_inc(dst_in, 16)

            def load_group(first):
                def body(g, slot):
                    if not (isinstance(g, int) and g < RING):
                        sp.wait_ge(added if first == 0 else eT_low, PAIRS * (g - RING + 1))
                    if first == 0:
                        sp.dma_start(e_sb[slot % RING], edge_rows(g)).then_inc(e_in[slot % RING], 16)
                    else:
                        sp.dma_start(eT_sb[slot % RING], edge_columns(g)).then_inc(e_in[slot % RING], 16)
                    if not (isinstance(g, int) and g < 2 * RING):
                        sp.wait_ge(pair_summed, PAIRS * (first + g - 2 * RING + 1))
                    if not (first == 0 and isinstance(g, int) and g == 0):
                        sp.dma_start(src_sb[slot][:], edge_ends(src, g)).then_inc(src_in[slot], 16)
                return body

            for g in range(RING):
                load_group(0)(g, g)
            for tile, array in ((w1T_sb, w1T), (w2T_sb, w2T), (w1m_sb, w1m), (w2m_sb, w2m), (w1u_sb, w1u), (w2u_sb, w2u)):
                sp.dma_start(tile[:], array.rearrange("(k p) m -> p k m", p=P)).then_inc(consts_in, 16)
            sp.dma_start(vt_sb[:], vt).then_inc(consts_in, 16)
            sp.dma_start(vr_sb[:], vr.partition_broadcast(P)).then_inc(consts_in, 16)
            for g in range(RING, 2 * RING):
                load_group(0)(g, g)
            run_groups(sp, load_group(0), 2 * RING, G - 1, 2 * RING)
            load_group(0)(G - 1, (G - 1) % (2 * RING))

            def node_a(s):
                if at := s.at(0):
                    c, n0, m = at
                    earlier(sp, a_h, c, 2)
                    earlier(sp, a_xc, c, 2)
                    waits_end(sp)
                    sp.dma_start(xt_n[m % 2], nodes_T(xT, n0)).then_inc(xt_in[m % 2], 16)
                if at := s.at(4):
                    c, n0, m = at
                    sp.wait_ge(a_x1, BLK * (c + 1))
                    last_store_but_one(sp, x1_out, c)
                    waits_end(sp)
                    sp.dma_start(node_rows(x1_dram, n0), x1_n[m % 2]).then_inc(x1_out[m % 2], 16)
                if at := s.at(5):
                    c, n0, m = at
                    sp.wait_ge(a_x1Ts, c + 1)
                    last_store_but_one(sp, x1T_out, c)
                    waits_end(sp)
                    sp.dma_start(nodes_T(x1T_dram, n0), x1T_n[m % 2]).then_inc(x1T_out[m % 2], 16)
                if at := s.at(6):
                    c, n0, m = at
                    sp.wait_ge(a_yr, c + 1)
                    last_store_but_one(sp, y_out, c)
                    waits_end(sp)
                    sp.dma_start(node_rows(y_dram, n0), y_n[m % 2]).then_inc(y_out[m % 2], 16)

            sp.wait_ge(added, PAIRS * G)
            run_steps(sp, node_a, C, N, 6)
            sp.wait_ge(a_yr, C)
            for q in range(2):
                sp.wait_ge(x1_out[q], 16 * slot_uses(C, q, 2))
                sp.wait_ge(x1T_out[q], 16 * slot_uses(C, q, 2))
            for g in range(2 * RING):
                load_group(G)(g, g)
            run_groups(sp, load_group(G), 2 * RING, G - 1, 2 * RING)
            load_group(G)(G - 1, (G - 1) % (2 * RING))

            sp.wait_ge(eT_low, PAIRS * G)

            def node_b(s):
                if at := s.at(0):
                    c, n0, m = at
                    earlier(sp, b_xb, c, 2)
                    waits_end(sp)
                    sp.dma_start(x1_n[m % 2], node_rows(x1_dram, n0)).then_inc(x1_in[m % 2], 16)
                if at := s.at(1):
                    c, n0, m = at
                    earlier(sp, b_r, c, 2)
                    waits_end(sp)
                    sp.dma_start(xt_n[m % 2], nodes_T(x1T_dram, n0)).then_inc(x1T_in[m % 2], 16)
                if at := s.at(5):
                    c, n0, m = at
                    sp.wait_ge(b_o, BLK * (c + 1))
                    last_store_but_one(sp, o_out, c)
                    waits_end(sp)
                    sp.dma_start(node_rows(out, n0), o_n[m % 2]).then_inc(o_out[m % 2], 16)

            run_steps(sp, node_b, C, N, 5)
            for q in range(2):
                sp.wait_ge(o_out[q], 16 * slot_uses(C, q, 2))
                sp.wait_ge(y_out[q], 16 * slot_uses(C, q, 2))

        @block.gpsimd
        def _(pool):
            def gather(table, first, uses_before):
                def body(g, slot):
                    pool.wait_ge(src_in[slot], nth_in_slot(g, slot, 2 * RING, 16) + 16 * uses_before(slot))
                    if not (first == 0 and isinstance(g, int) and g < RING):
                        pool.wait_ge(pair_summed, PAIRS * (first + g - RING + 1))
                    pool.sem_inc(gather_go, 1)
                    for u in range(TILES):
                        pool.indirect_dma_start(
                            out=m_sb[slot % RING][:, u, :], out_offset=None, in_=table,
                            in_offset=bass.IndirectOffsetOnAxis(ap=src_sb[slot][:, u:u + 1], axis=0),
                        ).then_inc(m_in[slot % RING], 16)
                return body

            pool.iota(iota_i[:], pattern=[[1, WIN]], base=0, channel_multiplier=0).then_inc(consts_made, 1)
            pool.iota(place_i[:], pattern=[[1, TILES]], base=0, channel_multiplier=TILES).then_inc(consts_made, 1)
            pool.memset(root[:], -0.5).then_inc(consts_made, 1)
            pool.memset(eps_t[:], EPS).then_inc(consts_made, 1)
            pool.memset(ident[:], 0.0).then_inc(consts_made, 1)
            pool.wait_ge(consts_made, 5)
            pool.affine_select(out=ident[:], in_=ident[:], compare_op=ALU.not_equal, fill=1.0, base=0,
                               pattern=[[-1, P]], channel_multiplier=1).then_inc(consts_made, 1)
            for g in range(RING):
                gather(x, 0, lambda slot: 0)(g, g)
            run_groups(pool, gather(x, 0, lambda slot: 0), RING, G, 2 * RING)

            pool.wait_ge(var_made, 1)
            pool.tensor_tensor(bn_r[:, 0, :], bn_r[:, 0, :], root[:], ALU.pow).then_inc(root_made, 1)
            pool.tensor_tensor(bn_r[:, 1, :], bn_r[:, 1, :], root[:], ALU.pow).then_inc(root_made, 1)

            def rstd(c, m, which, mv_sem, used, ve_sem, rs_sem):
                pool.wait_ge(mv_sem, BLK * (c + 1))
                if not (isinstance(c, int) and c < 2):
                    pool.wait_ge(used, BLK * (c - 1))
                r = rs_n[m % 2][:, which, :]
                pool.tensor_tensor(r, mv_n[m % 2][:, which, :, 1], eps_t[:], ALU.add).then_inc(ve_sem, 1)
                pool.wait_ge(ve_sem, c + 1)
                pool.tensor_tensor(r, r, root[:], ALU.pow).then_inc(rs_sem, 1)

            def node_a(s):
                if at := s.at(4):
                    c, n0, m = at
                    rstd(c, m, 0, a_mv, a_x1, a_ve, a_rs)

            run_steps(pool, node_a, C, N, 4)
            pool.wait_ge(a_h, C)
            pool.memset(acc[:, 0:KD, :], 0.0).then_inc(acc_zero, 1)
            for q in range(2):
                pool.wait_ge(y_out[q], 16 * slot_uses(C, q, 2))
            run_groups(pool, gather(y_dram, G, lambda slot: slot_uses(G, slot, 2 * RING)), 0, G, 2 * RING)

            def node_b(s):
                if at := s.at(5):
                    c, n0, m = at
                    rstd(c, m, 1, b_mv2, b_o, b_ve2, b_rs2)
                if at := s.at(3):
                    c, n0, m = at
                    rstd(c, m, 0, b_mv, b_n, b_ve, b_rs)
                if at := s.at(1):
                    c, n0, m = at
                    if isinstance(c, int) and c == 0:
                        pool.wait_ge(pair_summed, PAIRS * 2 * G)
                    pool.wait_ge(x1_in[m % 2], nth_in_slot(c, m % 2, 2, 16))
                    earlier(pool, b_s, c, 4)
                    pool.tensor_tensor(xb_n[m], x1_n[m % 2], row("beta"), ALU.add).then_inc(b_xb, 1)
                if at := s.at(4):
                    c, n0, m = at
                    pool.wait_ge(b_n, BLK * (c + 1))
                    pool.tensor_tensor(n_n[m % 2], n_n[m % 2], row("gamma"), ALU.mult).then_inc(b_ng, 1)
                    pool.wait_ge(b_ng, c + 1)
                    pool.tensor_tensor(n_n[m % 2], n_n[m % 2], xb_n[m], ALU.add).then_inc(b_s, 1)

            run_steps(pool, node_b, C, N, 5)

        @block.scalar
        def _(act):
            act.wait_ge(general_made, 1)
            is_general = act.value_load(general[0:1, 0:1], min_val=0, max_val=1)

            def activate(first, g, slot, j, func, split):
                n = PAIRS * (first + g) + j
                act.wait_ge(added, n + 1)
                v = m_sb[slot][:, 2 * j:2 * j + 2, :].rearrange("p t d -> p (t d)")
                if split:
                    if not (first == 0 and isinstance(g, int) and g < 1):
                        act.wait_ge(pair_summed, n - PAIRS + 1)
                    act.activation(m_hi[j][:], v, func).then_inc(act_high, 1)
                act.activation(v, v, func).then_inc(act_made, 1)

            def copy_sums(first, g, slot):
                act.wait_ge(pair_summed, PAIRS * (first + g + 1))
                if not (first == 0 and isinstance(g, int) and g < 2):
                    act.wait_ge(sum_turned, first + g - 1)
                act.copy(sum_n[slot % 2][:], bank[slot % 2][0:WIN, 0:D]).then_inc(sum_copied, 1)

            def first_pass(g, slot, sums=True, split=True):
                if sums:
                    copy_sums(0, g - 2, slot - 2)
                for j in range(PAIRS):
                    activate(0, g, slot, j, ACT.Relu, split)

            def first_pass_general(g, slot):
                first_pass(g, slot, sums=False, split=False)

            with act.If(is_general > 0):
                run_groups(act, first_pass_general, 0, G)
            with act.Else():
                first_pass(0, 0, sums=False)
                first_pass(1, 1, sums=False)
                first_pass(2, 2)
                first_pass(3, 3)
                run_groups(act, first_pass, 4, G)
                copy_sums(0, G - 2, G - 2)
                copy_sums(0, G - 1, G - 1)
            act.wait_ge(bn_made, 1)

            def node_a(s):
                if at := s.at(1):
                    c, n0, m = at
                    act.wait_ge(xt_in[m % 2], nth_in_slot(c, m % 2, 2, 16))
                    earlier(act, a_u, c, 4)
                    if isinstance(c, int) and c == 0:
                        act.wait_ge(pair_summed, PAIRS * G)
                    for k in range(KD):
                        last = act.activation(xc_n[m][:, k, :], xt_n[m % 2][:, k, :], ACT.Identity, bias=bn_c[:, 1, k:k + 1])
                    last.then_inc(a_xc, 1)
                    act.wait_ge(a_h, c + 1)
                    earlier(act, a_z1, c, 2)
                    for k in range(KD):
                        last = act.activation(f_n[m % 2][:, k, :], h_n[m][:, k, :], ACT.Identity,
                                              bias=bn_c[:, 0, k:k + 1], scale=bn_s[:, 0, k:k + 1])
                    last.then_inc(a_f, 1)
                if at := s.at(2):
                    c, n0, m = at
                    act.wait_ge(a_z1, c + 1)
                    earlier(act, a_z2, c, 2)
                    for k in range(KD):
                        last = act.activation(g_n[m % 2][:, k, :], bank[2][:, k * CHUNK:(k + 1) * CHUNK], ACT.Gelu,
                                              bias=vec("L0_b1", k))
                    last.then_inc(a_g, 1)
                if at := s.at(5):
                    c, n0, m = at
                    act.wait_ge(a_x1T, c + 1)
                    earlier(act, a_y, c, 2)
                    stored(act, x1T_out, c, m)
                    act.copy(x1T_n[m % 2], bank[5][:].rearrange("p (k n) -> p k n", k=KD)).then_inc(a_x1Ts, 1)

            run_steps(act, node_a, C, N, 5)

            def high_part(g, slot, j):
                if j == 0:
                    act.wait_ge(e_in[slot % RING],
                                nth_in_slot(g, slot % RING, RING, 16) + 16 * slot_uses(G, slot % RING, RING))
                if not (isinstance(g, int) and g < 1):
                    act.wait_ge(z_made, PAIRS * (g - 1) + j + 1)
                act.copy(eT_hi[j][:].rearrange("p (k t e) -> p k t e", k=KD, t=2), pair_of(eT_sb[slot % RING], j)
                         ).then_inc(eT_high, 1)

            def second_pass(g, slot, sums=True, ahead=True, split=True):
                if sums:
                    copy_sums(G, g - 2, slot - 2)
                for j in range(PAIRS):
                    if ahead:
                        high_part(g + 1, slot + 1, j)
                    activate(G, g, slot, j, ACT.Gelu, split)

            def second_pass_general(g, slot):
                second_pass(g, slot, sums=False, split=False)

            for j in range(PAIRS):
                high_part(0, 0, j)
            with act.If(is_general > 0):
                run_groups(act, second_pass_general, 0, G - 1)
                second_pass(G - 1, (G - 1) % RING, sums=False, ahead=False, split=False)
            with act.Else():
                second_pass(0, 0, sums=False)
                second_pass(1, 1, sums=False)
                run_groups(act, second_pass, 2, G - 1)
                second_pass(G - 1, (G - 1) % RING, ahead=False)
                copy_sums(G, G - 2, G - 2)
                copy_sums(G, G - 1, G - 1)

            def node_b(s):
                if at := s.at(1):
                    c, n0, m = at
                    act.wait_ge(b_v, c + 1)
                    earlier(act, b_w, c, 2)
                    for k in range(KH):
                        z = bank[3 + k // KD][:, k % KD * CHUNK:(k % KD + 1) * CHUNK]
                        last = act.activation(g_n[m % 2][:, k, :], z, ACT.Gelu,
                                              bias=vec("b1u_lo" if k < KD else "b1u_hi", k % KD))
                    last.then_inc(b_g, 1)

            run_steps(act, node_b, C, N, 1)

        @block.tensor
        def _(pe):
            def sum_tiles(psum, selection, slot, tiles, degrees=None):
                for u in tiles:
                    if degrees is not None:
                        pe.matmul(psum[:, DEG:DEG + WIN], ones_b[:], degrees[:, u, :],
                                  start=(u == 0), stop=(u == TILES - 1), skip_group_check=True)
                    last = pe.matmul(psum[:, 0:D], selection[:, u, :].bitcast(F32), m_sb[slot][:, u, :],
                                     start=(u == 0 and degrees is None), stop=(u == TILES - 1), skip_group_check=True)
                return last

            def turn_sums(psum, sums):
                for k in range(KD):
                    last = pe.matmul(psum[:, D + k * WIN:D + (k + 1) * WIN], sums[:, k * P:(k + 1) * P],
                                     ident[0:WIN, 0:WIN], start=True, stop=True, is_transpose=True, skip_group_check=True)
                return last

            def sum_all_windows(first, g, slot, degrees=None):
                pe.sem_inc(gen_go, 1)
                with pe.Fori(0, NW) as k:
                    n = (g + first) * NW + k
                    pe.wait_ge(gen_sel, n + 1)
                    pe.wait_ge(gen_acc, n + 1)
                    sum_tiles(bank[0], sel[0], slot, range(TILES), degrees).then_inc(gen_seg, 1)
                    pe.wait_ge(gen_copied, n + 1)
                    waits_end(pe)
                    turn_sums(bank[0], sum_n[0]).then_inc(gen_turned, 1)
                pe.wait_ge(gen_seg, (g + first + 1) * NW)
                pe.sem_inc(pair_summed, PAIRS)

            pe.wait_ge(win_ready, 1)
            pe.matmul(bank[7][:, 0:G], ones[0:1, :], win_f[:], start=True, stop=True).then_inc(win_spread, 1)
            pe.wait_ge(extent_ready, 1)
            pe.matmul(bank[6][:, 0:1], ones[:], extent[:, 2:3], start=True, stop=True).then_inc(counted, 1)
            pe.wait_ge(general_made, 1)
            pe.wait_ge(consts_made, 6)
            is_general = pe.value_load(general[0:1, 0:1], min_val=0, max_val=1)

            def turn_group(first, g, slot):
                pe.wait_ge(sum_copied, first + g + 1)
                waits_end(pe)
                turn_sums(bank[slot % 2], sum_n[slot % 2]).then_inc(sum_turned, 1)

            def pair_sums(first, g, slot, j):
                pe.wait_ge(act_low, PAIRS * (first + g) + j + 1)
                if j == 0:
                    pe.wait_ge(sel_made, first + g + 1)
                    pe.wait_ge(acc_done, first + g + 1)
                psum, degrees = bank[slot % 2], first == 0
                for t in range(2):
                    u = 2 * j + t
                    if degrees:
                        pe.matmul(psum[:, DEG:DEG + WIN], ones_b[:], sel_b[slot % 2][:, u, :],
                                  start=(u == 0), stop=(u == TILES - 1), skip_group_check=True)
                    for part in (m_lo, m_hi):
                        last = pe.matmul(psum[:, 0:D], sel[slot % 2][:, u, :], part[j][:, t * D:(t + 1) * D],
                                         start=(u == 0 and part is m_lo and not degrees),
                                         stop=(u == TILES - 1 and part is m_hi), skip_group_check=True)
                last.then_inc(pair_summed, 1)

            def first_pass(g, slot, turned_sums=True):
                for j in range(PAIRS):
                    pair_sums(0, g - 1, slot - 1, j)
                    if j == 1 and turned_sums:
                        turn_group(0, g - 2, slot - 2)

            def first_pass_general(g, slot):
                pe.wait_ge(act_made, PAIRS * (g + 1))
                sum_all_windows(0, g, slot, sel_b[0])

            with pe.If(is_general > 0):
                run_groups(pe, first_pass_general, 0, G)
            with pe.Else():
                first_pass(1, 1, turned_sums=False)
                run_groups(pe, first_pass, 2, G + 1)
                turn_group(0, G - 1, G - 1)

            pe.wait_ge(consts_in, 16 * 8)

            def dense(psum, weights, values, ks, ms, width=CHUNK):
                for i, m in enumerate(ms):
                    for k in ks:
                        last = pe.matmul(psum[:, i * width:(i + 1) * width], weights[:, k, m * P:(m + 1) * P],
                                         values(k), start=(k == 0), stop=(k == len(ks) - 1))
                return last

            def transposes(psum, values, last=None):
                for a in range(2):
                    for b in range(2):
                        last = pe.transpose(psum[:, (2 * b + a) * P:(2 * b + a + 1) * P],
                                            values[:, a, b * P:(b + 1) * P], ident[:])
                return last

            def node_a(s):
                if at := s.at(2):
                    c, n0, m = at
                    pe.wait_ge(a_f, c + 1)
                    earlier(pe, a_g, c, 1)
                    dense(bank[2], w1T_sb, lambda k: f_n[m % 2][:, k, :], range(KD), range(KD)).then_inc(a_z1, 1)
                if at := s.at(3):
                    c, n0, m = at
                    pe.wait_ge(a_g, c + 1)
                    earlier(pe, a_t, c, 1)
                    dense(bank[3], w2T_sb, lambda k: g_n[m % 2][:, k, :], range(KD), range(KD)).then_inc(a_z2, 1)
                if at := s.at(4):
                    c, n0, m = at
                    pe.wait_ge(a_u, c + 1)
                    if not (isinstance(c, int) and c < 1):
                        pe.wait_ge(a_x1, BLK * c)
                    transposes(bank[4], u_n[m % 2]).then_inc(a_uT, 1)
                if at := s.at(5):
                    c, n0, m = at
                    pe.wait_ge(a_x1, BLK * (c + 1))
                    earlier(pe, a_x1Ts, c, 1)
                    transposes(bank[5], x1_n[m % 2]).then_inc(a_x1T, 1)
                if at := s.at(6):
                    c, n0, m = at
                    pe.wait_ge(a_x1Ts, c + 1)
                    earlier(pe, a_yr, c, 1)
                    for b in range(BLK):
                        for k in range(KD):
                            last = pe.matmul(bank[6][:, b * D:(b + 1) * D], x1T_n[m % 2][:, k, b * P:(b + 1) * P],
                                             w1m_sb[:, k, :], start=(k == 0), stop=(k == KD - 1))
                    last.then_inc(a_y, 1)

            run_steps(pe, node_a, C, N, 6)
            pe.wait_ge(a_yr, C)

            pe.wait_ge(w_split, 2)

            def product(g, slot, j):
                pe.wait_ge(eT_low, PAIRS * g + j + 1)
                if not (isinstance(g, int) and g < 2):
                    pe.wait_ge(added, PAIRS * (G + g - 2) + j + 1)
                parts = ((eT_lo, w1m_hi), (eT_hi, w1m_lo), (eT_hi, w1m_hi))
                for t in range(2):
                    for i, (a, w) in enumerate(parts):
                        for k in range(KD):
                            last = pe.matmul(z_bank(slot, j)[:, t * D:(t + 1) * D],
                                             a[j][:, (k * 2 + t) * P:(k * 2 + t + 1) * P], w[:, k, :],
                                             start=(i == 0 and k == 0), stop=(i == len(parts) - 1 and k == KD - 1))
                last.then_inc(z_made, 1)

            def second_pass(g, slot, turned_sums=True):
                for j in range(PAIRS):
                    product(g, slot, j)
                    pair_sums(G, g - 1, slot - 1, j)
                    if j == 1 and turned_sums:
                        turn_group(G, g - 2, slot - 2)

            def second_pass_general(g, slot):
                for j in range(PAIRS):
                    product(g, slot, j)
                pe.wait_ge(act_made, PAIRS * (G + g))
                sum_all_windows(G, g - 1, (slot - 1) % RING)

            for j in range(PAIRS):
                product(0, 0, j)
            with pe.If(is_general > 0):
                run_groups(pe, second_pass_general, 1, G)
                pe.wait_ge(act_made, PAIRS * 2 * G)
                sum_all_windows(G, G - 1, (G - 1) % RING)
            with pe.Else():
                second_pass(1, 1, turned_sums=False)
                run_groups(pe, second_pass, 2, G)
                turn_group(G, G - 2, G - 2)
                for j in range(PAIRS):
                    pair_sums(G, G - 1, G - 1, j)
                turn_group(G, G - 1, G - 1)

            pe.wait_ge(acc_done, 2 * G + 2)

            def node_b(s):
                if at := s.at(0):
                    c, n0, m = at
                    if not (isinstance(c, int) and c < 1):
                        pe.wait_ge(b_q1, KD * c)
                    dense(bank[2], w2m_sb, lambda k: acc[:, k, bass.ds(n0, CHUNK)], range(KD), range(KD)).then_inc(b_q, 1)
                if at := s.at(1):
                    c, n0, m = at
                    pe.wait_ge(b_q2, c + 1)
                    earlier(pe, b_g, c, 1)
                    dense(bank[3], w1u_sb, lambda k: q_n[m % 2][:, k, :], range(KD), range(0, KD))
                    dense(bank[4], w1u_sb, lambda k: q_n[m % 2][:, k, :], range(KD), range(KD, KH)).then_inc(b_v, 1)
                if at := s.at(2):
                    c, n0, m = at
                    pe.wait_ge(b_g, c + 1)
                    earlier(pe, b_r, c, 1)
                    dense(bank[5], w2u_sb, lambda k: g_n[m % 2][:, k, :], range(KH), range(KD)).then_inc(b_w, 1)
                if at := s.at(3):
                    c, n0, m = at
                    pe.wait_ge(b_r, c + 1)
                    if not (isinstance(c, int) and c < 1):
                        pe.wait_ge(b_n, BLK * c)
                    transposes(bank[6], r_n[m % 2]).then_inc(b_rT, 1)

            run_steps(pe, node_b, C, N, 3)

        @block.vector
        def _(dve):
            steps = [0]

            def link(instruction):
                steps[0] += 1
                instruction.then_inc(prep, 1)
                dve.wait_ge(prep, steps[0])

            dve.sem_inc(acc_done, 2)
            dve.sem_inc(gen_acc, 1)
            for s in range(2):
                dve.memset(sel[s][:].bitcast(F32), 0.0)
            dve.memset(ones_b[:], 1.0)
            link(dve.memset(ones[:], 1.0))
            dve.wait_ge(dst_in, 16 * (4 if G > full else 2))
            dve.tensor_copy(win_f[:], win_i[:]).then_inc(win_ready, 1)
            link(dve.tensor_copy(dst_f[:], dst_i[:]))
            dve.wait_ge(consts_made, 4)
            link(dve.tensor_copy(iota[:], iota_i[:]))
            if repeated:
                link(dve.tensor_scalar(repeat[:], place_i[:], float(repeated), OUTSIDE, ALU.is_lt, ALU.mult))
            dve.wait_ge(win_spread, 1)
            link(dve.tensor_copy(win_bc[:], bank[7][:, 0:G]))
            link(dve.tensor_tensor(rel[:], dst_f[:], win_bc[:].unsqueeze(2).broadcast_to([P, G, TILES]), ALU.subtract))
            dve.tensor_reduce(extent[:, 0:1], rel[:].rearrange("p g u -> p (g u)"), AX_X, ALU.min)
            link(dve.tensor_reduce(extent[:, 1:2], rel[:].rearrange("p g u -> p (g u)"), AX_X, ALU.max))
            link(dve.tensor_scalar(extent[:, 3:4], extent[:, 1:2], float(WIN - 1), None, ALU.is_gt))
            link(dve.tensor_scalar(extent[:, 0:1], extent[:, 0:1], 0.0, None, ALU.is_lt))
            dve.tensor_tensor(extent[:, 2:3], extent[:, 0:1], extent[:, 3:4], ALU.max).then_inc(extent_ready, 1)
            dve.wait_ge(counted, 1)
            dve.tensor_scalar(general[:], bank[6][:, 0:1], 1.0, None, ALU.min).then_inc(general_made, 1)
            if repeated:
                link(dve.tensor_tensor(rel[:, G - 1, :], rel[:, G - 1, :], repeat[:], ALU.add))
                link(dve.tensor_tensor(dst_f[:, G - 1, :], dst_f[:, G - 1, :], repeat[:], ALU.add))
            dve.memset(acc[:], 0.0).then_inc(acc_zero, 1)
            dve.wait_ge(general_made, 1)
            is_general = dve.value_load(general[0:1, 0:1], min_val=0, max_val=1)

            def select(s, positions):
                return dve.tensor_tensor(s, iota[:].unsqueeze(1).broadcast_to([P, TILES, WIN]),
                                         positions.unsqueeze(2).broadcast_to([P, TILES, WIN]), ALU.is_equal)

            def selection(first, g, slot):
                if not (first == 0 and isinstance(g, int) and g < 2):
                    dve.wait_ge(pair_summed, PAIRS * (first + g - 1))
                positions = rel[:, bass.ds(g, 1), :].rearrange("p a u -> p (a u)")
                if first == 0:
                    select(sel_b[slot % 2][:], positions)
                select(sel[slot % 2][:, :, 0:WIN], positions).then_inc(sel_made, 1)

            def accumulate(psum, w, rows, done):
                at_w = acc[:, 0:rows, bass.ds(w, WIN)]
                dve.tensor_tensor(at_w, at_w, psum[:, D:D + rows * WIN].rearrange("p (k n) -> p k n", n=WIN),
                                  ALU.add).then_inc(done, 1)

            def accumulate_group(first, g, slot, rows):
                w = dve.value_load(win_i[0:1, bass.ds(g, 1)], min_val=0, max_val=N - 1)
                dve.wait_ge(sum_turned, first + g + 1)
                dve.wait_ge(acc_done, first + g + 2)
                accumulate(bank[slot % 2], w, rows, acc_done)

            def all_windows(first, g, rows):
                made = (g + first) * (NW + 1)
                dve.wait_ge(acc_done, first + g + 2)
                dve.tensor_copy(rel_k[:], dst_f[:, bass.ds(g, 1), :].rearrange("p a u -> p (a u)")).then_inc(gen_rel, 1)
                with dve.Fori(0, NW) as k:
                    n = (g + first) * NW + k
                    dve.wait_ge(gen_rel, made + k + 1)
                    if first == 0:
                        select(sel_b[0][:], rel_k[:])
                    select(sel[0][:, :, 0:WIN], rel_k[:]).then_inc(gen_sel, 1)
                    dve.wait_ge(gen_sel, n + 1)
                    dve.tensor_scalar(rel_k[:], rel_k[:], float(-WIN), None, ALU.add).then_inc(gen_rel, 1)
                    dve.wait_ge(gen_seg, n + 1)
                    dve.tensor_copy(sum_n[0][:], bank[0][0:WIN, 0:D]).then_inc(gen_copied, 1)
                    dve.wait_ge(gen_turned, n + 1)
                    accumulate(bank[0], k * WIN, rows, gen_acc)
                dve.wait_ge(gen_acc, (g + first + 1) * NW + 1)
                dve.sem_inc(acc_done, 1)

            def low_part(first, g, slot, j):
                n = PAIRS * (first + g) + j
                dve.wait_ge(act_high, n + 1)
                dve.wait_ge(act_made, n + 1)
                v = m_sb[slot % RING][:, 2 * j:2 * j + 2, :].rearrange("p t d -> p (t d)")
                dve.tensor_tensor(m_lo[j][:], v, m_hi[j][:].bitcast(F32), ALU.subtract).then_inc(act_low, 1)

            def add_edges(g, slot, j):
                if j == 0:
                    dve.wait_ge(e_in[slot], nth_in_slot(g, slot, RING, 16))
                    dve.wait_ge(m_in[slot], nth_in_slot(g, slot, RING, 16 * TILES))
                v = m_sb[slot][:, 2 * j:2 * j + 2, :]
                dve.tensor_tensor(v, v, e_sb[slot][:, 2 * j:2 * j + 2, :], ALU.add).then_inc(added, 1)

            def first_pass(g, slot, low=True, sums=True):
                for j in range(PAIRS):
                    if low:
                        low_part(0, g - 1, slot - 1, j)
                    add_edges(g, slot, j)
                    if j == 1:
                        selection(0, g, slot)
                        if sums:
                            accumulate_group(0, g - 2, slot - 2, KD + 1)

            def first_pass_general(g, slot):
                for j in range(PAIRS):
                    add_edges(g, slot, j)
                all_windows(0, g, KD + 1)

            dve.wait_ge(acc_zero, 1)
            with dve.If(is_general > 0):
                run_groups(dve, first_pass_general, 0, G)
            with dve.Else():
                first_pass(0, 0, low=False, sums=False)
                first_pass(1, 1, sums=False)
                run_groups(dve, first_pass, 2, G)
                for j in range(PAIRS):
                    low_part(0, G - 1, G - 1, j)
                for g in range(G - 2, G):
                    accumulate_group(0, g, g, KD + 1)

            dve.wait_ge(consts_in, 16 * 8)
            dve.tensor_copy(w1m_hi[:], w1m_sb[:]).then_inc(w_split, 1)
            dve.wait_ge(w_split, 1)
            dve.tensor_tensor(w1m_lo[:], w1m_sb[:], w1m_hi[:].bitcast(F32), ALU.subtract).then_inc(w_split, 1)

            v = {name: vt_sb[:, VT.index(name), :] for name in VT}
            dve.tensor_scalar(bn_r[:, 0, :], v["bn1_var"], EPS, None, ALU.add)
            dve.tensor_scalar(bn_r[:, 1, :], v["bn2_var"], EPS, None, ALU.add).then_inc(var_made, 1)
            dve.wait_ge(root_made, 2)
            link(dve.tensor_tensor(bn_s[:, 0, :], bn_r[:, 0, :], v["bn1_gamma"], ALU.mult))
            link(dve.tensor_tensor(bn_s[:, 1, :], bn_r[:, 1, :], v["bn2_gamma"], ALU.mult))
            link(dve.tensor_tensor(bn_t[:, 0, :], bn_s[:, 0, :], v["bn1_mean"], ALU.mult))
            link(dve.tensor_tensor(bn_c[:, 0, :], v["bn1_beta"], bn_t[:, 0, :], ALU.subtract))
            link(dve.tensor_tensor(bn_t[:, 1, :], v["L0_b2"], v["bn2_mean"], ALU.subtract))
            link(dve.tensor_tensor(bn_t[:, 1, :], bn_t[:, 1, :], bn_s[:, 1, :], ALU.mult))
            dve.tensor_tensor(bn_c[:, 1, :], bn_t[:, 1, :], v["bn2_beta"], ALU.add).then_inc(bn_made, 1)
            dve.wait_ge(bn_made, 1)
            dve.wait_ge(acc_done, G + 2)

            def statistics(m, which, values, c, st_sem, mv_sem, ve_sem):
                for b in range(BLK):
                    dve.bn_stats(st_n[m % 2][:, which, b, :], values(b)).then_inc(st_sem, 1)
                if not (isinstance(c, int) and c < 2):
                    dve.wait_ge(ve_sem, c - 1)
                dve.wait_ge(st_sem, BLK * (c + 1))
                waits_end(dve)
                for b in range(BLK):
                    dve.bn_aggr(mv_n[m % 2][:, which, b, :], st_n[m % 2][:, which, b, :]).then_inc(mv_sem, 1)

            def norm(m, which, to, values, c, mv_sem, rs_sem, done):
                dve.wait_ge(mv_sem, BLK * (c + 1))
                dve.wait_ge(rs_sem, c + 1)
                for b in range(BLK):
                    dve.tensor_scalar(to[:, b, :], values(b), mv_n[m % 2][:, which, b, 0:1],
                                      rs_n[m % 2][:, which, b:b + 1], ALU.subtract, ALU.mult).then_inc(done, 1)

            def node_a(s):
                if at := s.at(1):
                    c, n0, m = at
                    dve.wait_ge(xt_in[m % 2], nth_in_slot(c, m % 2, 2, 16))
                    earlier(dve, a_f, c, 4)
                    dve.scalar_tensor_tensor(out=h_n[m], in0=xt_n[m % 2], scalar=2.0,
                                             in1=acc[:, 0:KD, bass.ds(n0, CHUNK)], op0=ALU.mult, op1=ALU.add
                                             ).then_inc(a_h, 1)
                if at := s.at(3):
                    c, n0, m = at
                    dve.wait_ge(a_z2, c + 1)
                    dve.wait_ge(a_h, c + 1)
                    dve.tensor_tensor(h_n[m], bank[3][:].rearrange("p (k n) -> p k n", k=KD), h_n[m], ALU.add
                                      ).then_inc(a_t, 1)
                if at := s.at(4):
                    c, n0, m = at
                    dve.wait_ge(a_uT, c + 1)
                    statistics(m, 0, lambda b: bank[4][:, b * D:(b + 1) * D], c, a_st, a_mv, a_ve)
                if at := s.at(3):
                    c, n0, m = at
                    dve.wait_ge(a_t, c + 1)
                    dve.wait_ge(a_xc, c + 1)
                    earlier(dve, a_uT, c, 2)
                    for k in range(KD):
                        last = dve.scalar_tensor_tensor(out=u_n[m % 2][:, k, :], in0=h_n[m][:, k, :],
                                                        scalar=bn_s[:, 1, k:k + 1], in1=xc_n[m][:, k, :],
                                                        op0=ALU.mult, op1=ALU.add)
                    last.then_inc(a_u, 1)
                if at := s.at(6):
                    c, n0, m = at
                    dve.wait_ge(a_y, c + 1)
                    stored(dve, y_out, c, m)
                    dve.tensor_tensor(y_n[m % 2], bank[6][:].rearrange("p (b d) -> p b d", d=D), row("b1m"), ALU.add
                                      ).then_inc(a_yr, 1)
                if at := s.at(4):
                    c, n0, m = at
                    stored(dve, x1_out, c, m)
                    earlier(dve, a_x1T, c, 2)
                    norm(m, 0, x1_n[m % 2], lambda b: bank[4][:, b * D:(b + 1) * D], c, a_mv, a_rs, a_x1)

            run_steps(dve, node_a, C, N, 6)
            dve.wait_ge(acc_zero, 2)

            def add_rows(g, slot, j):
                if j == 0:
                    dve.wait_ge(m_in[slot], nth_in_slot(g, slot, RING, 16 * TILES)
                                + 16 * TILES * slot_uses(G, slot, RING))
                dve.wait_ge(z_made, PAIRS * g + j + 1)
                v2 = m_sb[slot][:, 2 * j:2 * j + 2, :]
                dve.tensor_tensor(v2, z_bank(slot, j)[:].rearrange("p (t d) -> p t d", d=D), v2, ALU.add
                                  ).then_inc(added, 1)

            def eT_low_part(g, slot, j):
                dve.wait_ge(eT_high, PAIRS * g + j + 1)
                hi, lo = (part[j][:].rearrange("p (k t e) -> p k t e", k=KD, t=2) for part in (eT_hi, eT_lo))
                dve.tensor_tensor(lo, pair_of(eT_sb[slot % RING], j), hi.bitcast(F32), ALU.subtract
                                  ).then_inc(eT_low, 1)

            def second_pass(g, slot, low=True, ahead=True, sums=True):
                for j in range(PAIRS):
                    add_rows(g, slot, j)
                    if j == PAIRS - 1:
                        low_part(G, g, slot, 0)
                    elif low:
                        low_part(G, g - 1, slot - 1, j + 1)
                    if j == 1:
                        selection(G, g, slot)
                        if sums:
                            accumulate_group(G, g - 2, slot - 2, KD)
                    if ahead:
                        eT_low_part(g + 1, slot + 1, j)

            def second_pass_general(g, slot):
                for j in range(PAIRS):
                    add_rows(g, slot, j)
                    eT_low_part(g + 1, slot + 1, j)
                all_windows(G, g - 1, KD)

            for j in range(PAIRS):
                eT_low_part(0, 0, j)
            with dve.If(is_general > 0):
                for j in range(PAIRS):
                    add_rows(0, 0, j)
                    eT_low_part(1, 1, j)
                run_groups(dve, second_pass_general, 1, G - 1)
                for j in range(PAIRS):
                    add_rows(G - 1, (G - 1) % RING, j)
                all_windows(G, G - 2, KD)
                all_windows(G, G - 1, KD)
            with dve.Else():
                second_pass(0, 0, low=False, sums=False)
                second_pass(1, 1, sums=False)
                run_groups(dve, second_pass, 2, G - 1)
                second_pass(G - 1, (G - 1) % RING, ahead=False)
                for j in range(1, PAIRS):
                    low_part(G, G - 1, G - 1, j)
                for g in range(G - 2, G):
                    accumulate_group(G, g, g, KD)
            dve.wait_ge(acc_done, 2 * G + 2)

            def node_b(s):
                if at := s.at(5):
                    c, n0, m = at
                    dve.wait_ge(b_s, c + 1)
                    statistics(m, 1, lambda b: n_n[m % 2][:, b, :], c, b_st2, b_mv2, b_ve2)
                if at := s.at(0):
                    c, n0, m = at
                    degree = acc[:, KD, bass.ds(n0, CHUNK)]
                    dve.tensor_scalar(f_n[m % 2][:, 0, :], degree, 1.0, None, ALU.max).then_inc(b_dm, 1)
                    dve.wait_ge(b_dm, c + 1)
                    dve.reciprocal(f_n[m % 2][:, 1, :], f_n[m % 2][:, 0, :]).then_inc(b_rd, 1)
                if at := s.at(5):
                    c, n0, m = at
                    stored(dve, o_out, c, m)
                    norm(m, 1, o_n[m % 2], lambda b: n_n[m % 2][:, b, :], c, b_mv2, b_rs2, b_o)
                if at := s.at(3):
                    c, n0, m = at
                    dve.wait_ge(b_rT, c + 1)
                    statistics(m, 0, lambda b: bank[6][:, b * D:(b + 1) * D], c, b_st, b_mv, b_ve)
                if at := s.at(0):
                    c, n0, m = at
                    degree = acc[:, KD, bass.ds(n0, CHUNK)]
                    dve.wait_ge(b_q, c + 1)
                    earlier(dve, b_v, c, 2)
                    for k in range(KD):
                        dve.scalar_tensor_tensor(out=q_n[m % 2][:, k, :], in0=degree, scalar=vec("b2m", k),
                                                 in1=bank[2][:, k * CHUNK:(k + 1) * CHUNK], op0=ALU.mult, op1=ALU.add
                                                 ).then_inc(b_q1, 1)
                if at := s.at(2):
                    c, n0, m = at
                    dve.wait_ge(b_w, c + 1)
                    dve.wait_ge(x1T_in[m % 2], nth_in_slot(c, m % 2, 2, 16))
                    earlier(dve, b_rT, c, 2)
                    for k in range(KD):
                        last = dve.scalar_tensor_tensor(out=r_n[m % 2][:, k, :], in0=bank[5][:, k * CHUNK:(k + 1) * CHUNK],
                                                        scalar=vec("b2u", k), in1=xt_n[m % 2][:, k, :],
                                                        op0=ALU.add, op1=ALU.add)
                    last.then_inc(b_r, 1)
                if at := s.at(0):
                    c, n0, m = at
                    dve.wait_ge(b_q1, KD * (c + 1))
                    dve.wait_ge(b_rd, c + 1)
                    dve.tensor_tensor(q_n[m % 2], q_n[m % 2],
                                      f_n[m % 2][:, 1:2, :].broadcast_to([P, KD, CHUNK]), ALU.mult).then_inc(b_q2, 1)
                if at := s.at(3):
                    c, n0, m = at
                    norm(m, 0, n_n[m % 2], lambda b: bank[6][:, b * D:(b + 1) * D], c, b_mv, b_rs, b_n)

            run_steps(dve, node_b, C, N, 5)


def kernel(**inputs):
    import concourse.bacc as bacc
    from concourse.bass_utils import run_bass_kernel_spmd

    a = {k: np.asarray(v) for k, v in inputs.items()}
    names = {"L0_b1": "L0_gnn_b1", "L0_b2": "L0_gnn_b2", "b2m": "L1_gnn_b2m", "b2u": "L1_gnn_b2u"}
    per_feature = [a[names.get(n, "L0_gnn_" + n)] for n in VT[:-2]]
    per_feature += [a["L1_gnn_b1u"][0:D], a["L1_gnn_b1u"][D:2 * D]]
    arrays = {
        "x": a["x"], "xT": a["x"].T, "src": a["src"], "dst": a["dst"], "edge": a["edge_attr_256"],
        "edgeT": a["edge_attr_256"].T,
        "w1T": a["L0_gnn_W1"].T, "w2T": a["L0_gnn_W2"].T, "w1m": a["L1_gnn_W1m"], "w2m": a["L1_gnn_W2m"],
        "w1u": a["L1_gnn_W1u"], "w2u": a["L1_gnn_W2u"],
        "vt": np.stack(per_feature).reshape(len(VT), KD, P).transpose(2, 0, 1),
        "vr": np.stack([a["L1_gnn_b1m"], a["L1_gnn_gamma"], a["L1_gnn_beta"]]),
    }
    arrays = {k: np.ascontiguousarray(v) for k, v in arrays.items()}
    nc = bacc.Bacc("TRN2", target_bir_lowering=False, num_devices=1)
    args = {k: nc.dram_tensor(f"in_{k}", v.shape, mybir.dt.from_np(v.dtype), kind="ExternalInput").ap()
            for k, v in arrays.items()}
    out = nc.dram_tensor("out", list(a["x"].shape), F32, kind="ExternalOutput").ap()
    build(nc, *args.values(), out)
    result = run_bass_kernel_spmd(nc, [{f"in_{k}": v for k, v in arrays.items()}], core_ids=[0])
    return result.results[0]["out"]
```

```python
from contextlib import ExitStack

import numpy as np

import concourse.bass as bass
from concourse import mybir

ALU = mybir.AluOpType
ACT = mybir.ActivationFunctionType
AX_X = mybir.AxisListType.X
F32 = mybir.dt.float32
F32R = mybir.dt.float32r
BF16 = mybir.dt.bfloat16
I32 = mybir.dt.int32

P = 128
D = 256
KD = D // P
TILES = 6
PAIRS = TILES // 2
GROUP = TILES * P
WIN = 64
RING = 4
CHUNK = 256
BLK = CHUNK // P
STEPS = 4
EPS = 1e-5
OUTSIDE = -1.0e6

VT = ["L0_b1", "L0_b2", "bn1_gamma", "bn1_beta", "bn1_mean", "bn1_var",
      "bn2_gamma", "bn2_beta", "bn2_mean", "bn2_var", "b2m", "b2u", "b1u_lo", "b1u_hi"]
VR = ["b1m", "gamma", "beta"]


class Step:

    def __init__(self, i, phase, chunks, nodes):
        self.i, self.phase, self.chunks, self.nodes = i, phase, chunks, nodes

    def at(self, offset):
        c = self.i - offset
        if isinstance(self.i, int):
            if not 0 <= c < self.chunks:
                return None
            return c, min(c * CHUNK, self.nodes - CHUNK), c % STEPS
        return c, c * CHUNK, (self.phase - offset) % STEPS


def run_steps(eng, body, chunks, nodes, depth):
    first = 2 * STEPS
    rounds = max(0, (chunks - 1 - first) // STEPS)
    for i in range(min(first, chunks + depth)):
        body(Step(i, i % STEPS, chunks, nodes))
    if rounds:
        with eng.Fori(0, rounds) as r:
            for s in range(STEPS):
                body(Step(r * STEPS + (first + s), s, chunks, nodes))
    for i in range(first + rounds * STEPS, chunks + depth):
        body(Step(i, i % STEPS, chunks, nodes))


def run_groups(eng, body, start, stop, ring=RING):
    rounds = (stop - start) // ring
    if rounds:
        with eng.Fori(0, rounds) as r:
            for s in range(ring):
                body(r * ring + (start + s), (start + s) % ring)
    for g in range(start + rounds * ring, stop):
        body(g, g % ring)


def build(nc, x, xT, src, dst, edge, edgeT, w1T, w2T, w1m, w2mT, w1u, w2u, vt, vr, out):
    N = x.shape[0]
    E = edge.shape[0]
    full = E // GROUP
    G = -(-E // GROUP)
    repeated = G * GROUP - E
    NW = -(-N // WIN)
    NPAD = N + WIN
    C = -(-N // CHUNK)
    H2 = w1u.shape[1]
    KH = H2 // P
    DEG = D + KD * WIN
    assert 2 * RING < full and G <= 512 and C >= 2 and KH == 2 * KD

    y_dram = nc.dram_tensor("y_scratch", [N, D], F32, kind="Internal").ap()
    x1_dram = nc.dram_tensor("x1_scratch", [N, D], F32, kind="Internal").ap()
    x1T_dram = nc.dram_tensor("x1T_scratch", [D, N], F32, kind="Internal").ap()

    with ExitStack() as ctx:
        def sb(name, shape, dt=F32):
            return ctx.enter_context(nc.sbuf_tensor(name, shape, dt))

        def sem(name):
            return ctx.enter_context(nc.semaphore(name))

        def sems(name, n):
            return [sem(f"{name}{i}") for i in range(n)]

        bank = [ctx.enter_context(nc.psum_tensor(f"bank{i}", [P, 512], F32)) for i in range(8)]

        acc = sb("acc", [P, KD + 1, NPAD])
        e_all = sb("e_all", [P, RING * TILES * D])
        e_sb = [e_all[:, s * TILES * D:(s + 1) * TILES * D].rearrange("p (u d) -> p u d", d=D)
                for s in range(RING)]
        eT_sb = [e_all[:, s * TILES * D:(s + 1) * TILES * D].rearrange("p (k e) -> p k e", k=KD)
                 for s in range(RING)]
        m_all = sb("m_all", [P, RING * TILES * D])
        m_sb = [m_all[:, s * TILES * D:(s + 1) * TILES * D].rearrange("p (u d) -> p u d", d=D)
                for s in range(RING)]
        src_sb = [sb(f"src{s}", [P, TILES], I32) for s in range(2 * RING)]
        eT_hi, eT_lo, m_hi, m_lo = ([sb(f"{n}{j}", [P, 2 * D], F32R) for j in range(PAIRS)]
                                    for n in ("eT_hi", "eT_lo", "m_hi", "m_lo"))
        sel = [sb(f"sel{s}", [P, TILES, P], F32R) for s in range(2)]
        sel_b = [sb(f"sel_b{s}", [P, TILES, WIN], BF16) for s in range(2)]
        sum_n = [sb(f"sum_n{s}", [WIN, D]) for s in range(2)]
        dst_i = acc[:, 0, 0:G * TILES].rearrange("p (g u) -> p g u", u=TILES).bitcast(I32)
        rel = sb("rel", [P, G, TILES])
        win_i = sb("win_i", [1, G], I32)
        win_f = sb("win_f", [1, G])
        win_bc = sb("win_bc", [P, G])
        iota_i = sb("iota_i", [P, WIN], I32)
        iota = sb("iota", [P, WIN])
        place_i = sb("place_i", [P, TILES], I32)
        repeat = sb("repeat", [P, TILES])
        extent = sb("extent", [P, 4])
        general = sb("general", [P, 1], I32)
        rel_k = sb("rel_k", [P, TILES])
        zero = sb("zero", [P, 1])
        ones = sb("ones", [P, P])
        ones_b = sb("ones_b", [P, P], BF16)
        ident = sb("ident", [P, P])
        root = sb("root", [P, BLK])
        eps_t = sb("eps_t", [P, BLK])
        minus = sb("minus", [P, BLK])
        w1T_sb = sb("w1T_sb", [P, KD, D])
        w2T_sb = sb("w2T_sb", [P, KD, D])
        w1m_sb = sb("w1m_sb", [P, KD, D])
        w1m_hi = sb("w1m_hi", [P, KD, D], F32R)
        w1m_lo = sb("w1m_lo", [P, KD, D], F32R)
        w2mT_sb = sb("w2mT_sb", [P, KD, D])
        w1u_sb = sb("w1u_sb", [P, KD, H2])
        w2u_sb = sb("w2u_sb", [P, KH, D])
        wmu_hi, wmu_lo = (sb(n, [P, KD, H2], F32R) for n in ("wmu_hi", "wmu_lo"))
        w2u_hi, w2u_lo = (sb(n, [P, KH, D], F32R) for n in ("w2u_hi", "w2u_lo"))
        bmu_hi, bmu_lo = (sb(n, [1, H2], F32R) for n in ("bmu_hi", "bmu_lo"))
        some = [w1m_hi[0:1, i, :] for i in range(2)]
        vt_sb = sb("vt_sb", [P, len(VT), KD])
        vr_sb = sb("vr_sb", [P, len(VR), D])
        bn_r = sb("bn_r", [P, 2, KD])
        bn_s = sb("bn_s", [P, 2, KD])
        bn_c = sb("bn_c", [P, 2, KD])
        bn_t = sb("bn_t", [P, 2, KD])

        def vec(name, k):
            return vt_sb[:, VT.index(name), k:k + 1]

        def row(name):
            return vr_sb[:, VR.index(name), :].unsqueeze(1).broadcast_to([P, BLK, D])

        UNIT = KD * CHUNK

        def spare(first, n, inner=CHUNK, of=m_all, units=1):
            return [of[:, (first + i * units) * UNIT:(first + (i + 1) * units) * UNIT]
                    .rearrange("p (k n) -> p k n", n=inner) for i in range(n)]

        h_n = spare(0, 4)
        xc_n = spare(4, 4)
        u_n = spare(8, 2)
        y_n = spare(10, 2, D)
        q_n = spare(0, 2)
        r_n = spare(2, 2)
        xb_n = spare(4, 4, D)
        n_n = spare(8, 2, D)
        o_n = spare(10, 2, D)
        xt_n = spare(0, 2, of=e_all)
        deg_n, rec_n = (spare(i, 1, of=e_all)[0][:, 0, :] for i in (10, 11))
        f_n = spare(2, 2, of=e_all) 
        x1_n = spare(4, 2, D, of=e_all)
        g_n = spare(6, 2, of=e_all, units=KH // KD)
        x1T_n = [g_n[i][:, KD:KH, :] for i in range(2)]
        q_hi, q_lo = eT_hi[0:2], eT_lo[0:2]
        g_hi = [[m_hi[0], m_hi[1]], [m_hi[2], eT_hi[2]]]
        g_lo = [[m_lo[0], m_lo[1]], [m_lo[2], eT_lo[2]]]
        nb_n = [sb(f"nb_n{i}", [P, BLK]) for i in range(2)]
        st_n = [sb(f"st_n{i}", [P, 2, BLK, 6]) for i in range(2)]
        mv_n = [sb(f"mv_n{i}", [P, 2, BLK, 2]) for i in range(2)]
        rs_n = [sb(f"rs_n{i}", [P, 2, BLK]) for i in range(2)]

        dst_in = sem("dst_in")
        vt_in = sem("vt_in")
        consts_in = sem("consts_in")
        consts_made = sem("consts_made")
        prep = sem("prep")
        win_ready = sem("win_ready")
        win_spread = sem("win_spread")
        extent_ready = sem("extent_ready")
        counted = sem("counted")
        general_made = sem("general_made")
        var_made = sem("var_made")
        root_made = sem("root_made")
        bn_made = sem("bn_made")
        e_in = sems("e_in", RING)
        src_in = sems("src_in", 2 * RING)
        m_in = sems("m_in", RING)
        gather_go = sem("gather_go")
        sel_made = sem("sel_made")
        sum_copied = sem("sum_copied")
        sum_turned = sem("sum_turned")
        acc_done = sem("acc_done")
        gen_go = sem("gen_go")
        gen_rel = sem("gen_rel")
        gen_sel = sem("gen_sel")
        gen_seg = sem("gen_seg")
        gen_copied = sem("gen_copied")
        gen_turned = sem("gen_turned")
        gen_acc = sem("gen_acc")
        eT_high = sem("eT_high")
        eT_low = sem("eT_low")
        z_made = sem("z_made")
        added = sem("added")
        act_high = sem("act_high")
        act_made = sem("act_made")
        act_low = sem("act_low")
        pair_summed = sem("pair_summed")
        waited = {e: sem(f"waited_{e.name}") for e in (nc.sync.engine, nc.vector.engine, nc.tensor.engine)}
        w_split = sem("w_split")
        w_fused = sem("w_fused")
        w_high = sem("w_high")
        acc_zero = sem("acc_zero")

        (a_d, a_id, a_rd, a_mn, a_nb, a_h, a_xc, a_f, a_z1, a_g, a_z2, a_t, a_u, a_uT, a_st, a_mv, a_ve, a_rs, a_x1, a_x1T,
         a_x1Ts, a_y, a_yr) = map(sem, (
            "a_d", "a_id", "a_rd", "a_mn", "a_nb", "a_h", "a_xc", "a_f", "a_z1", "a_g", "a_z2", "a_t", "a_u", "a_uT", "a_st", "a_mv", "a_ve",
            "a_rs", "a_x1", "a_x1T", "a_x1Ts", "a_y", "a_yr"))
        xt_in, x1_out, x1T_out, y_out = (sems(n, 2) for n in ("xt_in", "x1_out", "x1T_out", "y_out"))
        (b_q, b_qh, b_ql, b_v, b_gh, b_g, b_gl, b_w, b_r, b_rT, b_st, b_mv, b_ve, b_rs, b_n, b_xb,
         b_ng, b_s, b_st2, b_mv2, b_ve2, b_rs2, b_mn2, b_nb, b_o) = map(sem, (
            "b_q", "b_qh", "b_ql", "b_v", "b_gh", "b_g", "b_gl", "b_w", "b_r", "b_rT", "b_st", "b_mv", "b_ve",
            "b_rs", "b_n", "b_xb", "b_ng", "b_s", "b_st2", "b_mv2", "b_ve2", "b_rs2", "b_mn2", "b_nb", "b_o"))
        x1T_in, x1_in, o_out = (sems(n, 2) for n in ("x1T_in", "x1_in", "o_out"))

        block = ctx.enter_context(nc.Block())

        def edge_rows(g):
            if isinstance(g, int) and g >= full:
                return edge[E - GROUP:E, :].rearrange("(p u) d -> p u d", u=TILES)
            return edge[0:full * GROUP, :].rearrange("(g p u) d -> g p u d", p=P, u=TILES)[g]

        def edge_columns(g):
            if isinstance(g, int) and g >= full:
                return edgeT[:, E - GROUP:E].rearrange("(k p) e -> p k e", p=P)
            return edgeT[:, 0:full * GROUP].rearrange("(k p) (g e) -> g p k e", p=P, e=GROUP)[g]

        def pair_of(eT, j):
            return eT.rearrange("p k (e u) -> p k u e", u=TILES)[:, :, 2 * j:2 * j + 2, :]

        def edge_ends(array, g):
            if isinstance(g, int) and g >= full:
                return array[E - GROUP:E].rearrange("(p u) -> p u", u=TILES)
            return array[0:full * GROUP].rearrange("(g p u) -> g p u", p=P, u=TILES)[g]

        def z_bank(slot, j):
            return bank[2 + slot % 2 * PAIRS + j]

        def nodes_T(array, n0):
            return array.rearrange("(k p) n -> p k n", p=P)[:, :, bass.ds(n0, CHUNK)]

        def node_rows(array, n0):
            return array[bass.ds(n0, CHUNK), :].rearrange("(b p) d -> p b d", p=P)

        def slot_uses(n, slot, ring):
            return (n - slot + ring - 1) // ring

        def nth_in_slot(n, slot, ring, each):
            return (n - slot) * (each // ring) + each

        def earlier(eng, semaphore, c, ring):
            if not (isinstance(c, int) and c < ring):
                eng.wait_ge(semaphore, c - ring + 1)

        def waits_end(eng):
            eng.sem_inc(waited[eng.engine], 1)

        def last_store_but_one(eng, semaphores, c):
            if isinstance(c, int) and c == C - 1:
                q = (C - 2) % 2
                eng.wait_ge(semaphores[q], 16 * slot_uses(C - 1, q, 2))

        def stored(eng, semaphores, c, m):
            if not (isinstance(c, int) and c < 2):
                eng.wait_ge(semaphores[m % 2], nth_in_slot(c, m % 2, 2, 16) - 16)

        @block.sync
        def _(sp):
            sp.dma_start(src_sb[0][:], edge_ends(src, 0)).then_inc(src_in[0], 16)
            sp.dma_start(vt_sb[:], vt).then_inc(vt_in, 16)
            sp.dma_start(win_i[:, 0:full], dst[0:full * GROUP].rearrange("(a g e) -> a g e", a=1, e=GROUP)[:, :, 0],
                         allow_slow_non_contiguous=True
                         ).then_inc(dst_in, 16)
            sp.dma_start(dst_i[:, 0:full, :], dst[0:full * GROUP].rearrange("(g p u) -> p g u", p=P, u=TILES)
                         ).then_inc(dst_in, 16)
            if G > full:
                sp.dma_start(win_i[:, full:G], dst[E - GROUP:E - GROUP + 1].rearrange("(a b) -> a b", a=1)
                             ).then_inc(dst_in, 16)
                sp.dma_start(dst_i[:, full, :], edge_ends(dst, full)).then_inc(dst_in, 16)
            for g in range(1, RING):
                sp.dma_start(src_sb[g][:], edge_ends(src, g)).then_inc(src_in[g], 16)

            def load_group(first):
                def body(g, slot):
                    if not (isinstance(g, int) and g < RING):
                        sp.wait_ge(added if first == 0 else eT_low, PAIRS * (g - RING + 1))
                    if first == 0:
                        sp.dma_start(e_sb[slot % RING], edge_rows(g)).then_inc(e_in[slot % RING], 16)
                    else:
                        sp.dma_start(eT_sb[slot % RING], edge_columns(g)).then_inc(e_in[slot % RING], 16)
                    if not (isinstance(g, int) and g < 2 * RING):
                        sp.wait_ge(pair_summed, PAIRS * (first + g - 2 * RING + 1))
                    if not (first == 0 and isinstance(g, int) and g < RING):
                        sp.dma_start(src_sb[slot][:], edge_ends(src, g)).then_inc(src_in[slot], 16)
                return body

            for g in range(RING):
                load_group(0)(g, g)
            for g in range(RING, 2 * RING):
                load_group(0)(g, g)
            for tile, array in ((w1T_sb, w1T), (w2T_sb, w2T), (w1m_sb, w1m), (w2mT_sb, w2mT), (w1u_sb, w1u), (w2u_sb, w2u)):
                sp.dma_start(tile[:], array.rearrange("(k p) m -> p k m", p=P)).then_inc(consts_in, 16)
            sp.dma_start(vr_sb[:], vr.partition_broadcast(P)).then_inc(consts_in, 16)
            run_groups(sp, load_group(0), 2 * RING, G - 1, 2 * RING)
            load_group(0)(G - 1, (G - 1) % (2 * RING))

            def node_a(s):
                if at := s.at(0):
                    c, n0, m = at
                    earlier(sp, a_h, c, 2)
                    earlier(sp, a_xc, c, 2)
                    waits_end(sp)
                    sp.dma_start(xt_n[m % 2], nodes_T(xT, n0)).then_inc(xt_in[m % 2], 16)
                if at := s.at(4):
                    c, n0, m = at
                    sp.wait_ge(a_x1, BLK * (c + 1))
                    last_store_but_one(sp, x1_out, c)
                    waits_end(sp)
                    sp.dma_start(node_rows(x1_dram, n0), x1_n[m % 2]).then_inc(x1_out[m % 2], 16)
                if at := s.at(5):
                    c, n0, m = at
                    sp.wait_ge(a_x1Ts, c + 1)
                    last_store_but_one(sp, x1T_out, c)
                    waits_end(sp)
                    sp.dma_start(nodes_T(x1T_dram, n0), x1T_n[m % 2]).then_inc(x1T_out[m % 2], 16)
                if at := s.at(7):
                    c, n0, m = at
                    sp.wait_ge(a_yr, c + 1)
                    last_store_but_one(sp, y_out, c)
                    waits_end(sp)
                    sp.dma_start(node_rows(y_dram, n0), y_n[m % 2]).then_inc(y_out[m % 2], 16)

            sp.wait_ge(added, PAIRS * G)
            run_steps(sp, node_a, C, N, 7)
            sp.wait_ge(a_yr, C)
            for q in range(2):
                sp.wait_ge(x1_out[q], 16 * slot_uses(C, q, 2))
                sp.wait_ge(x1T_out[q], 16 * slot_uses(C, q, 2))
            for g in range(2 * RING):
                load_group(G)(g, g)
            run_groups(sp, load_group(G), 2 * RING, G - 1, 2 * RING)
            load_group(G)(G - 1, (G - 1) % (2 * RING))

            sp.wait_ge(eT_low, PAIRS * G)

            def node_b(s):
                if at := s.at(0):
                    c, n0, m = at
                    earlier(sp, b_xb, c, 2)
                    waits_end(sp)
                    sp.dma_start(x1_n[m % 2], node_rows(x1_dram, n0)).then_inc(x1_in[m % 2], 16)
                if at := s.at(2):
                    c, n0, m = at
                    earlier(sp, b_r, c, 2)
                    waits_end(sp)
                    sp.dma_start(xt_n[m % 2], nodes_T(x1T_dram, n0)).then_inc(x1T_in[m % 2], 16)
                if at := s.at(5):
                    c, n0, m = at
                    sp.wait_ge(b_o, BLK * (c + 1))
                    last_store_but_one(sp, o_out, c)
                    waits_end(sp)
                    sp.dma_start(node_rows(out, n0), o_n[m % 2]).then_inc(o_out[m % 2], 16)

            run_steps(sp, node_b, C, N, 5)
            for q in range(2):
                sp.wait_ge(o_out[q], 16 * slot_uses(C, q, 2))
                sp.wait_ge(y_out[q], 16 * slot_uses(C, q, 2))

        @block.gpsimd
        def _(pool):
            def gather(table, first, uses_before):
                def body(g, slot):
                    pool.wait_ge(src_in[slot], nth_in_slot(g, slot, 2 * RING, 16) + 16 * uses_before(slot))
                    if not (first == 0 and isinstance(g, int) and g < RING):
                        pool.wait_ge(pair_summed, PAIRS * (first + g - RING + 1))
                    pool.sem_inc(gather_go, 1)
                    for u in range(TILES):
                        pool.indirect_dma_start(
                            out=m_sb[slot % RING][:, u, :], out_offset=None, in_=table,
                            in_offset=bass.IndirectOffsetOnAxis(ap=src_sb[slot][:, u:u + 1], axis=0),
                        ).then_inc(m_in[slot % RING], 16)
                return body

            pool.iota(iota_i[:], pattern=[[1, WIN]], base=0, channel_multiplier=0).then_inc(consts_made, 1)
            pool.iota(place_i[:], pattern=[[1, TILES]], base=0, channel_multiplier=TILES).then_inc(consts_made, 1)
            pool.memset(root[:], -0.5).then_inc(consts_made, 1)
            pool.memset(eps_t[:], EPS).then_inc(consts_made, 1)
            pool.memset(ident[:], 0.0).then_inc(consts_made, 1)
            pool.memset(minus[:], -1.0).then_inc(consts_made, 1)
            pool.wait_ge(consts_made, 6)
            pool.affine_select(out=ident[:], in_=ident[:], compare_op=ALU.not_equal, fill=1.0, base=0,
                               pattern=[[-1, P]], channel_multiplier=1).then_inc(consts_made, 1)
            gather(x, 0, lambda slot: 0)(0, 0)
            pool.wait_ge(var_made, 1)
            pool.tensor_tensor(bn_r[:, 0, :], bn_r[:, 0, :], root[:], ALU.pow).then_inc(root_made, 1)
            pool.tensor_tensor(bn_r[:, 1, :], bn_r[:, 1, :], root[:], ALU.pow).then_inc(root_made, 1)
            for g in range(1, RING):
                gather(x, 0, lambda slot: 0)(g, g)
            run_groups(pool, gather(x, 0, lambda slot: 0), RING, G, 2 * RING)

            def rstd(c, m, which, mv_sem, used, ve_sem, rs_sem):
                pool.wait_ge(mv_sem, BLK * (c + 1))
                if not (isinstance(c, int) and c < 2):
                    pool.wait_ge(used, BLK * (c - 1))
                r = rs_n[m % 2][:, which, :]
                pool.tensor_tensor(r, mv_n[m % 2][:, which, :, 1], eps_t[:], ALU.add).then_inc(ve_sem, 1)
                pool.wait_ge(ve_sem, c + 1)
                pool.tensor_tensor(r, r, root[:], ALU.pow).then_inc(rs_sem, 1)

            def negative_mean(c, m, which, rs_sem, mn_sem, nb_sem):
                pool.wait_ge(rs_sem, c + 1)
                pool.tensor_tensor(nb_n[m % 2][:], mv_n[m % 2][:, which, :, 0], rs_n[m % 2][:, which, :], ALU.mult
                                   ).then_inc(mn_sem, 1)
                pool.wait_ge(mn_sem, c + 1)
                pool.tensor_tensor(nb_n[m % 2][:], nb_n[m % 2][:], minus[:], ALU.mult).then_inc(nb_sem, 1)

            def node_a(s):
                if at := s.at(4):
                    c, n0, m = at
                    rstd(c, m, 0, a_mv, a_x1, a_ve, a_rs)
                    negative_mean(c, m, 0, a_rs, a_mn, a_nb)

            run_steps(pool, node_a, C, N, 4)
            pool.wait_ge(a_h, C)
            pool.memset(acc[:, 0:KD, :], 0.0).then_inc(acc_zero, 1)
            for q in range(2):
                pool.wait_ge(y_out[q], 16 * slot_uses(C, q, 2))
            run_groups(pool, gather(y_dram, G, lambda slot: slot_uses(G, slot, 2 * RING)), 0, G, 2 * RING)

            def node_b(s):
                if at := s.at(4):
                    c, n0, m = at
                    rstd(c, m, 0, b_mv, b_n, b_ve, b_rs)
                if at := s.at(5):
                    c, n0, m = at
                    rstd(c, m, 1, b_mv2, b_o, b_ve2, b_rs2)
                    negative_mean(c, m, 1, b_rs2, b_mn2, b_nb)
                if at := s.at(2):
                    c, n0, m = at
                    if isinstance(c, int) and c == 0:
                        pool.wait_ge(pair_summed, PAIRS * 2 * G)
                    pool.wait_ge(x1_in[m % 2], nth_in_slot(c, m % 2, 2, 16))
                    earlier(pool, b_s, c, 4)
                    pool.tensor_tensor(xb_n[m], x1_n[m % 2], row("beta"), ALU.add).then_inc(b_xb, 1)
                if at := s.at(4):
                    c, n0, m = at
                    pool.wait_ge(b_n, BLK * (c + 1))
                    pool.tensor_tensor(n_n[m % 2], n_n[m % 2], row("gamma"), ALU.mult).then_inc(b_ng, 1)
                    pool.wait_ge(b_ng, c + 1)
                    pool.tensor_tensor(n_n[m % 2], n_n[m % 2], xb_n[m], ALU.add).then_inc(b_s, 1)

            run_steps(pool, node_b, C, N, 5)

        @block.scalar
        def _(act):
            act.wait_ge(acc_zero, 1)
            act.copy(acc[:, 1:KD + 1, :], zero[:].unsqueeze(2).broadcast_to([P, KD, NPAD])).then_inc(acc_zero, 1)
            act.wait_ge(general_made, 1)
            is_general = act.value_load(general[0:1, 0:1], min_val=0, max_val=1)

            def activate(first, g, slot, j, func, split):
                n = PAIRS * (first + g) + j
                act.wait_ge(added, n + 1)
                v = m_sb[slot][:, 2 * j:2 * j + 2, :].rearrange("p t d -> p (t d)")
                if split:
                    if not (first == 0 and isinstance(g, int) and g < 1):
                        act.wait_ge(pair_summed, n - PAIRS + 1)
                    act.activation(m_hi[j][:], v, func).then_inc(act_high, 1)
                act.activation(v, v, func).then_inc(act_made, 1)

            def copy_sums(first, g, slot):
                act.wait_ge(pair_summed, PAIRS * (first + g + 1))
                if not (first == 0 and isinstance(g, int) and g < 2):
                    act.wait_ge(sum_turned, first + g - 1)
                act.copy(sum_n[slot % 2][:], bank[slot % 2][0:WIN, 0:D]).then_inc(sum_copied, 1)

            def first_pass(g, slot, sums=True, split=True):
                if sums:
                    copy_sums(0, g - 2, slot - 2)
                for j in range(PAIRS):
                    activate(0, g, slot, j, ACT.Relu, split)

            def first_pass_general(g, slot):
                first_pass(g, slot, sums=False, split=False)

            with act.If(is_general > 0):
                run_groups(act, first_pass_general, 0, G)
            with act.Else():
                first_pass(0, 0, sums=False)
                first_pass(1, 1, sums=False)
                first_pass(2, 2)
                first_pass(3, 3)
                run_groups(act, first_pass, 4, G)
                copy_sums(0, G - 2, G - 2)
                copy_sums(0, G - 1, G - 1)
            act.wait_ge(bn_made, 1)

            def scaled_rows(m, which, to, values, done):
                for b in range(BLK):
                    act.activation(to[:, b, :], values(b), ACT.Identity, bias=nb_n[m % 2][:, b:b + 1],
                                   scale=rs_n[m % 2][:, which, b:b + 1]).then_inc(done, 1)

            def node_a(s):
                if at := s.at(1):
                    c, n0, m = at
                    act.wait_ge(xt_in[m % 2], nth_in_slot(c, m % 2, 2, 16))
                    earlier(act, a_u, c, 4)
                    if isinstance(c, int) and c == 0:
                        act.wait_ge(pair_summed, PAIRS * G)
                    for k in range(KD):
                        last = act.activation(xc_n[m][:, k, :], xt_n[m % 2][:, k, :], ACT.Identity, bias=bn_c[:, 1, k:k + 1])
                    last.then_inc(a_xc, 1)
                    act.wait_ge(a_h, c + 1)
                    earlier(act, a_z1, c, 2)
                    for k in range(KD):
                        last = act.activation(f_n[m % 2][:, k, :], h_n[m][:, k, :], ACT.Identity,
                                              bias=bn_c[:, 0, k:k + 1], scale=bn_s[:, 0, k:k + 1])
                    last.then_inc(a_f, 1)
                if at := s.at(5):
                    c, n0, m = at
                    act.wait_ge(a_x1T, c + 1)
                    earlier(act, a_y, c, 2)
                    stored(act, x1T_out, c, m)
                    act.copy(x1T_n[m % 2], bank[5][:].rearrange("p (k n) -> p k n", k=KD)).then_inc(a_x1Ts, 1)
                if at := s.at(2):
                    c, n0, m = at
                    act.wait_ge(a_z1, c + 1)
                    earlier(act, a_z2, c, 2)
                    for k in range(KD):
                        last = act.activation(g_n[m % 2][:, k, :], bank[2][:, k * CHUNK:(k + 1) * CHUNK], ACT.Gelu,
                                              bias=vec("L0_b1", k))
                    last.then_inc(a_g, 1)
                if at := s.at(4):
                    c, n0, m = at
                    stored(act, x1_out, c, m)
                    earlier(act, a_x1T, c, 2)
                    act.wait_ge(a_nb, c + 1)
                    scaled_rows(m, 0, x1_n[m % 2], lambda b: bank[4][:, b * D:(b + 1) * D], a_x1)

            run_steps(act, node_a, C, N, 5)
            act.wait_ge(w_fused, 1)
            for k in range(KD):
                act.copy(wmu_hi[:, k, :], bank[k][:]).then_inc(w_high, 1)
            act.copy(bmu_hi[:], bank[7][0:1, :]).then_inc(w_high, 1)
            act.copy(w2u_hi[:], w2u_sb[:]).then_inc(w_high, 1)

            def high_part(g, slot, j):
                if j == 0:
                    act.wait_ge(e_in[slot % RING],
                                nth_in_slot(g, slot % RING, RING, 16) + 16 * slot_uses(G, slot % RING, RING))
                if not (isinstance(g, int) and g < 1):
                    act.wait_ge(z_made, PAIRS * (g - 1) + j + 1)
                act.copy(eT_hi[j][:].rearrange("p (k t e) -> p k t e", k=KD, t=2), pair_of(eT_sb[slot % RING], j)
                         ).then_inc(eT_high, 1)

            def second_pass(g, slot, sums=True, ahead=True, split=True):
                if sums:
                    copy_sums(G, g - 2, slot - 2)
                for j in range(PAIRS):
                    if ahead:
                        high_part(g + 1, slot + 1, j)
                    activate(G, g, slot, j, ACT.Gelu, split)

            def second_pass_general(g, slot):
                second_pass(g, slot, sums=False, split=False)

            for j in range(PAIRS):
                high_part(0, 0, j)
            with act.If(is_general > 0):
                run_groups(act, second_pass_general, 0, G - 1)
                second_pass(G - 1, (G - 1) % RING, sums=False, ahead=False, split=False)
            with act.Else():
                second_pass(0, 0, sums=False)
                second_pass(1, 1, sums=False)
                run_groups(act, second_pass, 2, G - 1)
                second_pass(G - 1, (G - 1) % RING, ahead=False)
                copy_sums(G, G - 2, G - 2)
                copy_sums(G, G - 1, G - 1)

            def node_b(s):
                if at := s.at(0):
                    c, n0, m = at
                    act.wait_ge(b_q, c + 1)
                    earlier(act, b_v, c, 2)
                    act.copy(q_hi[m % 2][:], q_n[m % 2].rearrange("p k n -> p (k n)")).then_inc(b_qh, 1)
                if at := s.at(1):
                    c, n0, m = at
                    act.wait_ge(b_v, c + 1)
                    earlier(act, b_w, c, 2)
                    for to, done in ((g_hi, b_gh), (None, b_g)):
                        for k in range(KH):
                            i, cols = k // KD, slice(k % KD * CHUNK, (k % KD + 1) * CHUNK)
                            last = act.activation(g_n[m % 2][:, k, :] if to is None else to[m % 2][i][:, cols],
                                                  bank[m % 2 * 2 + i][:, cols], ACT.Gelu,
                                                  bias=vec(("b1u_lo", "b1u_hi")[i], k % KD))
                        last.then_inc(done, 1)
                if at := s.at(5):
                    c, n0, m = at
                    act.wait_ge(b_nb, c + 1)
                    stored(act, o_out, c, m)
                    scaled_rows(m, 1, o_n[m % 2], lambda b: n_n[m % 2][:, b, :], b_o)

            run_steps(act, node_b, C, N, 5)

        @block.tensor
        def _(pe):
            def sum_tiles(psum, selection, slot, tiles, degrees=None):
                for u in tiles:
                    if degrees is not None:
                        pe.matmul(psum[:, DEG:DEG + WIN], ones_b[:], degrees[:, u, :],
                                  start=(u == 0), stop=(u == TILES - 1), skip_group_check=True)
                    last = pe.matmul(psum[:, 0:D], selection[:, u, :].bitcast(F32), m_sb[slot][:, u, :],
                                     start=(u == 0 and degrees is None), stop=(u == TILES - 1), skip_group_check=True)
                return last

            def turn_sums(psum, sums):
                for k in range(KD):
                    last = pe.matmul(psum[:, D + k * WIN:D + (k + 1) * WIN], sums[:, k * P:(k + 1) * P],
                                     ident[0:WIN, 0:WIN], start=True, stop=True, is_transpose=True, skip_group_check=True)
                return last

            def sum_all_windows(first, g, slot, degrees=None):
                pe.sem_inc(gen_go, 1)
                with pe.Fori(0, NW) as k:
                    n = (g + first) * NW + k
                    pe.wait_ge(gen_sel, n + 1)
                    pe.wait_ge(gen_acc, n + 1)
                    sum_tiles(bank[0], sel[0], slot, range(TILES), degrees).then_inc(gen_seg, 1)
                    pe.wait_ge(gen_copied, n + 1)
                    waits_end(pe)
                    turn_sums(bank[0], sum_n[0]).then_inc(gen_turned, 1)
                pe.wait_ge(gen_seg, (g + first + 1) * NW)
                pe.sem_inc(pair_summed, PAIRS)

            pe.wait_ge(win_ready, 1)
            pe.matmul(bank[7][:, 0:G], ones[0:1, :], win_f[:], start=True, stop=True).then_inc(win_spread, 1)
            pe.wait_ge(extent_ready, 1)
            pe.matmul(bank[6][:, 0:1], ones[:], extent[:, 2:3], start=True, stop=True).then_inc(counted, 1)
            pe.wait_ge(general_made, 1)
            pe.wait_ge(consts_made, 7)
            is_general = pe.value_load(general[0:1, 0:1], min_val=0, max_val=1)

            def turn_group(first, g, slot):
                pe.wait_ge(sum_copied, first + g + 1)
                waits_end(pe)
                turn_sums(bank[slot % 2], sum_n[slot % 2]).then_inc(sum_turned, 1)

            def pair_sums(first, g, slot, j):
                pe.wait_ge(act_low, PAIRS * (first + g) + j + 1)
                if j == 0:
                    pe.wait_ge(sel_made, first + g + 1)
                    pe.wait_ge(acc_done, first + g + 1)
                psum, degrees = bank[slot % 2], first == 0
                for t in range(2):
                    u = 2 * j + t
                    if degrees:
                        pe.matmul(psum[:, DEG:DEG + WIN], ones_b[:], sel_b[slot % 2][:, u, :],
                                  start=(u == 0), stop=(u == TILES - 1), skip_group_check=True)
                    for part in (m_lo, m_hi):
                        last = pe.matmul(psum[:, 0:D], sel[slot % 2][:, u, :], part[j][:, t * D:(t + 1) * D],
                                         start=(u == 0 and part is m_lo and not degrees),
                                         stop=(u == TILES - 1 and part is m_hi), skip_group_check=True)
                last.then_inc(pair_summed, 1)

            def first_pass(g, slot, turned_sums=True):
                for j in range(PAIRS):
                    pair_sums(0, g - 1, slot - 1, j)
                    if j == 1 and turned_sums:
                        turn_group(0, g - 2, slot - 2)

            def first_pass_general(g, slot):
                pe.wait_ge(act_made, PAIRS * (g + 1))
                sum_all_windows(0, g, slot, sel_b[0])

            with pe.If(is_general > 0):
                run_groups(pe, first_pass_general, 0, G)
            with pe.Else():
                first_pass(1, 1, turned_sums=False)
                run_groups(pe, first_pass, 2, G + 1)
                turn_group(0, G - 1, G - 1)

            pe.wait_ge(consts_in, 16 * 7)
            pe.wait_ge(vt_in, 16)

            def dense(psum, weights, values, ks, ms, width=CHUNK):
                for i, m in enumerate(ms):
                    for k in ks:
                        last = pe.matmul(psum[:, i * width:(i + 1) * width], weights[:, k, m * P:(m + 1) * P],
                                         values(k), start=(k == 0), stop=(k == len(ks) - 1))
                return last

            def transposes(psum, values, last=None):
                for a in range(2):
                    for b in range(2):
                        last = pe.transpose(psum[:, (2 * b + a) * P:(2 * b + a + 1) * P],
                                            values[:, a, b * P:(b + 1) * P], ident[:])
                return last

            def node_a(s):
                if at := s.at(2):
                    c, n0, m = at
                    pe.wait_ge(a_f, c + 1)
                    earlier(pe, a_g, c, 1)
                    dense(bank[2], w1T_sb, lambda k: f_n[m % 2][:, k, :], range(KD), range(KD)).then_inc(a_z1, 1)
                if at := s.at(5):
                    c, n0, m = at
                    pe.wait_ge(a_x1, BLK * (c + 1))
                    earlier(pe, a_x1Ts, c, 1)
                    transposes(bank[5], x1_n[m % 2]).then_inc(a_x1T, 1)
                if at := s.at(4):
                    c, n0, m = at
                    pe.wait_ge(a_u, c + 1)
                    if not (isinstance(c, int) and c < 1):
                        pe.wait_ge(a_x1, BLK * c)
                    transposes(bank[4], u_n[m % 2]).then_inc(a_uT, 1)
                if at := s.at(3):
                    c, n0, m = at
                    pe.wait_ge(a_g, c + 1)
                    earlier(pe, a_t, c, 1)
                    dense(bank[3], w2T_sb, lambda k: g_n[m % 2][:, k, :], range(KD), range(KD)).then_inc(a_z2, 1)
                if at := s.at(6):
                    c, n0, m = at
                    pe.wait_ge(a_x1Ts, c + 1)
                    earlier(pe, a_yr, c, 2)
                    for b in range(BLK):
                        for k in range(KD):
                            last = pe.matmul(bank[6 + m % 2][:, b * D:(b + 1) * D], x1T_n[m % 2][:, k, b * P:(b + 1) * P],
                                             w1m_sb[:, k, :], start=(k == 0), stop=(k == KD - 1))
                    last.then_inc(a_y, 1)

            run_steps(pe, node_a, C, N, 6)
            pe.wait_ge(a_yr, C)

            for i in range(KD):
                for k in range(KD):
                    pe.matmul(bank[i][:], w2mT_sb[:, k, i * P:(i + 1) * P], w1u_sb[:, k, :],
                              start=(k == 0), stop=(k == KD - 1))
            for k in range(KD):
                last = pe.matmul(bank[7][0:1, :], vec("b2m", k), w1u_sb[:, k, :], start=(k == 0), stop=(k == KD - 1))
            last.then_inc(w_fused, 1)
            pe.wait_ge(w_split, 4)

            def product(g, slot, j):
                pe.wait_ge(eT_low, PAIRS * g + j + 1)
                if not (isinstance(g, int) and g < 2):
                    pe.wait_ge(added, PAIRS * (G + g - 2) + j + 1)
                parts = ((eT_lo, w1m_hi), (eT_hi, w1m_lo), (eT_hi, w1m_hi))
                for t in range(2):
                    for i, (a, w) in enumerate(parts):
                        for k in range(KD):
                            last = pe.matmul(z_bank(slot, j)[:, t * D:(t + 1) * D],
                                             a[j][:, (k * 2 + t) * P:(k * 2 + t + 1) * P], w[:, k, :],
                                             start=(i == 0 and k == 0), stop=(i == len(parts) - 1 and k == KD - 1))
                last.then_inc(z_made, 1)

            def second_pass(g, slot, turned_sums=True):
                for j in range(PAIRS):
                    product(g, slot, j)
                    pair_sums(G, g - 1, slot - 1, j)
                    if j == 1 and turned_sums:
                        turn_group(G, g - 2, slot - 2)

            def second_pass_general(g, slot):
                for j in range(PAIRS):
                    product(g, slot, j)
                pe.wait_ge(act_made, PAIRS * (G + g))
                sum_all_windows(G, g - 1, (slot - 1) % RING)

            for j in range(PAIRS):
                product(0, 0, j)
            with pe.If(is_general > 0):
                run_groups(pe, second_pass_general, 1, G)
                pe.wait_ge(act_made, PAIRS * 2 * G)
                sum_all_windows(G, G - 1, (G - 1) % RING)
            with pe.Else():
                second_pass(1, 1, turned_sums=False)
                run_groups(pe, second_pass, 2, G)
                turn_group(G, G - 2, G - 2)
                for j in range(PAIRS):
                    pair_sums(G, G - 1, G - 1, j)
                turn_group(G, G - 1, G - 1)

            pe.wait_ge(acc_done, 2 * G + 2)

            def dense_parts(psum, weights, values, blocks, m, more=()):
                hi, lo = weights
                v_hi, v_lo = values
                products = [(w[:, k, m * P:(m + 1) * P], v(k)) for w, v in ((hi, v_lo), (lo, v_hi), (hi, v_hi))
                            for k in range(blocks)] + list(more)
                for i, (w, v) in enumerate(products):
                    last = pe.matmul(psum, w, v, start=(i == 0), stop=(i == len(products) - 1))
                return last

            def node_b(s):
                if at := s.at(1):
                    c, n0, m = at
                    pe.wait_ge(b_ql, c + 1)
                    earlier(pe, b_g, c, 2)
                    q = [lambda k, part=part: part[m % 2][:, k * CHUNK:(k + 1) * CHUNK] for part in (q_hi, q_lo)]
                    for i in range(KH):
                        last = dense_parts(bank[m % 2 * 2 + i // KD][:, i % KD * CHUNK:(i % KD + 1) * CHUNK],
                                           (wmu_hi, wmu_lo), q, KD, i,
                                           [(b[:, i * P:(i + 1) * P], some[m % 2]) for b in (bmu_lo, bmu_hi)])
                    last.then_inc(b_v, 1)
                if at := s.at(2):
                    c, n0, m = at
                    pe.wait_ge(b_gl, c + 1)
                    earlier(pe, b_r, c, 2)
                    g = [lambda k, part=part: part[m % 2][k // KD][:, k % KD * CHUNK:(k % KD + 1) * CHUNK]
                         for part in (g_hi, g_lo)]
                    for i in range(KD):
                        last = dense_parts(bank[4 + m % 2][:, i * CHUNK:(i + 1) * CHUNK], (w2u_hi, w2u_lo), g, KH, i)
                    last.then_inc(b_w, 1)
                if at := s.at(3):
                    c, n0, m = at
                    pe.wait_ge(b_r, c + 1)
                    if not (isinstance(c, int) and c < 2):
                        pe.wait_ge(b_n, BLK * (c - 1))
                    transposes(bank[6 + m % 2], r_n[m % 2]).then_inc(b_rT, 1)

            run_steps(pe, node_b, C, N, 3)

        @block.vector
        def _(dve):
            steps = [0]

            def link(instruction):
                steps[0] += 1
                instruction.then_inc(prep, 1)
                dve.wait_ge(prep, steps[0])

            dve.sem_inc(acc_done, 2)
            dve.sem_inc(gen_acc, 1)
            dve.memset(zero[:], 0.0).then_inc(acc_zero, 1)
            for s in range(2):
                dve.memset(sel[s][:].bitcast(F32), 0.0)
            dve.memset(ones_b[:], 1.0)
            link(dve.memset(ones[:], 1.0))
            dve.wait_ge(vt_in, 16)
            v = {name: vt_sb[:, VT.index(name), :] for name in VT}
            dve.tensor_scalar(bn_r[:, 0, :], v["bn1_var"], EPS, None, ALU.add)
            dve.tensor_scalar(bn_r[:, 1, :], v["bn2_var"], EPS, None, ALU.add).then_inc(var_made, 1)
            dve.memset(acc[:, 0, G * TILES:NPAD], 0.0)
            dve.wait_ge(root_made, 2)
            link(dve.tensor_tensor(bn_s[:, 0, :], bn_r[:, 0, :], v["bn1_gamma"], ALU.mult))
            link(dve.tensor_tensor(bn_s[:, 1, :], bn_r[:, 1, :], v["bn2_gamma"], ALU.mult))
            link(dve.tensor_tensor(bn_t[:, 0, :], bn_s[:, 0, :], v["bn1_mean"], ALU.mult))
            link(dve.tensor_tensor(bn_c[:, 0, :], v["bn1_beta"], bn_t[:, 0, :], ALU.subtract))
            link(dve.tensor_tensor(bn_t[:, 1, :], v["L0_b2"], v["bn2_mean"], ALU.subtract))
            link(dve.tensor_tensor(bn_t[:, 1, :], bn_t[:, 1, :], bn_s[:, 1, :], ALU.mult))
            dve.tensor_tensor(bn_c[:, 1, :], bn_t[:, 1, :], v["bn2_beta"], ALU.add).then_inc(bn_made, 1)
            dve.wait_ge(bn_made, 1)
            dve.wait_ge(dst_in, 16 * (4 if G > full else 2))
            dve.tensor_copy(win_f[:], win_i[:]).then_inc(win_ready, 1)
            link(dve.tensor_copy(rel[:], dst_i[:]))
            dve.wait_ge(consts_made, 4)
            link(dve.tensor_copy(iota[:], iota_i[:]))
            if repeated:
                link(dve.tensor_scalar(repeat[:], place_i[:], float(repeated), OUTSIDE, ALU.is_lt, ALU.mult))
            dve.wait_ge(win_spread, 1)
            link(dve.tensor_copy(win_bc[:], bank[7][:, 0:G]))
            link(dve.tensor_tensor(rel[:], rel[:], win_bc[:].unsqueeze(2).broadcast_to([P, G, TILES]), ALU.subtract))
            dve.tensor_reduce(extent[:, 0:1], rel[:].rearrange("p g u -> p (g u)"), AX_X, ALU.min)
            link(dve.tensor_reduce(extent[:, 1:2], rel[:].rearrange("p g u -> p (g u)"), AX_X, ALU.max))
            link(dve.tensor_scalar(extent[:, 3:4], extent[:, 1:2], float(WIN - 1), None, ALU.is_gt))
            link(dve.tensor_scalar(extent[:, 0:1], extent[:, 0:1], 0.0, None, ALU.is_lt))
            dve.tensor_tensor(extent[:, 2:3], extent[:, 0:1], extent[:, 3:4], ALU.max).then_inc(extent_ready, 1)
            dve.wait_ge(counted, 1)
            dve.tensor_scalar(general[:], bank[6][:, 0:1], 1.0, None, ALU.min).then_inc(general_made, 1)
            if repeated:
                link(dve.tensor_tensor(rel[:, G - 1, :], rel[:, G - 1, :], repeat[:], ALU.add))
            dve.memset(acc[:, 0, 0:G * TILES], 0.0).then_inc(acc_zero, 1)
            dve.wait_ge(general_made, 1)
            is_general = dve.value_load(general[0:1, 0:1], min_val=0, max_val=1)

            def select(s, positions):
                return dve.tensor_tensor(s, iota[:].unsqueeze(1).broadcast_to([P, TILES, WIN]),
                                         positions.unsqueeze(2).broadcast_to([P, TILES, WIN]), ALU.is_equal)

            def selection(first, g, slot):
                if not (first == 0 and isinstance(g, int) and g < 2):
                    dve.wait_ge(pair_summed, PAIRS * (first + g - 1))
                positions = rel[:, bass.ds(g, 1), :].rearrange("p a u -> p (a u)")
                if first == 0:
                    select(sel_b[slot % 2][:], positions)
                select(sel[slot % 2][:, :, 0:WIN], positions).then_inc(sel_made, 1)

            def accumulate(psum, w, rows, done):
                at_w = acc[:, 0:rows, bass.ds(w, WIN)]
                dve.tensor_tensor(at_w, at_w, psum[:, D:D + rows * WIN].rearrange("p (k n) -> p k n", n=WIN),
                                  ALU.add).then_inc(done, 1)

            def accumulate_group(first, g, slot, rows):
                w = dve.value_load(win_i[0:1, bass.ds(g, 1)], min_val=0, max_val=N - 1)
                dve.wait_ge(sum_turned, first + g + 1)
                dve.wait_ge(acc_done, first + g + 2)
                accumulate(bank[slot % 2], w, rows, acc_done)

            def all_windows(first, g, rows):
                made = (g + first) * (NW + 1)
                dve.wait_ge(acc_done, first + g + 2)
                dve.tensor_tensor(rel_k[:], rel[:, bass.ds(g, 1), :].rearrange("p a u -> p (a u)"),
                                  win_bc[:, bass.ds(g, 1)].broadcast_to([P, TILES]), ALU.add).then_inc(gen_rel, 1)
                with dve.Fori(0, NW) as k:
                    n = (g + first) * NW + k
                    dve.wait_ge(gen_rel, made + k + 1)
                    if first == 0:
                        select(sel_b[0][:], rel_k[:])
                    select(sel[0][:, :, 0:WIN], rel_k[:]).then_inc(gen_sel, 1)
                    dve.wait_ge(gen_sel, n + 1)
                    dve.tensor_scalar(rel_k[:], rel_k[:], float(-WIN), None, ALU.add).then_inc(gen_rel, 1)
                    dve.wait_ge(gen_seg, n + 1)
                    dve.tensor_copy(sum_n[0][:], bank[0][0:WIN, 0:D]).then_inc(gen_copied, 1)
                    dve.wait_ge(gen_turned, n + 1)
                    accumulate(bank[0], k * WIN, rows, gen_acc)
                dve.wait_ge(gen_acc, (g + first + 1) * NW + 1)
                dve.sem_inc(acc_done, 1)

            def low_part(first, g, slot, j):
                n = PAIRS * (first + g) + j
                dve.wait_ge(act_high, n + 1)
                dve.wait_ge(act_made, n + 1)
                v = m_sb[slot % RING][:, 2 * j:2 * j + 2, :].rearrange("p t d -> p (t d)")
                dve.tensor_tensor(m_lo[j][:], v, m_hi[j][:].bitcast(F32), ALU.subtract).then_inc(act_low, 1)

            def add_edges(g, slot, j):
                if j == 0:
                    dve.wait_ge(e_in[slot], nth_in_slot(g, slot, RING, 16))
                    dve.wait_ge(m_in[slot], nth_in_slot(g, slot, RING, 16 * TILES))
                v = m_sb[slot][:, 2 * j:2 * j + 2, :]
                dve.tensor_tensor(v, v, e_sb[slot][:, 2 * j:2 * j + 2, :], ALU.add).then_inc(added, 1)

            def first_pass(g, slot, low=True, sums=True):
                for j in range(PAIRS):
                    if low:
                        low_part(0, g - 1, slot - 1, j)
                    add_edges(g, slot, j)
                    if j == 1:
                        selection(0, g, slot)
                        if sums:
                            accumulate_group(0, g - 2, slot - 2, KD + 1)

            def first_pass_general(g, slot):
                for j in range(PAIRS):
                    add_edges(g, slot, j)
                all_windows(0, g, KD + 1)

            dve.wait_ge(acc_zero, 3)
            with dve.If(is_general > 0):
                run_groups(dve, first_pass_general, 0, G)
            with dve.Else():
                first_pass(0, 0, low=False, sums=False)
                first_pass(1, 1, sums=False)
                run_groups(dve, first_pass, 2, G)
                for j in range(PAIRS):
                    low_part(0, G - 1, G - 1, j)
                for g in range(G - 2, G):
                    accumulate_group(0, g, g, KD + 1)

            dve.wait_ge(consts_in, 16 * 7)
            dve.wait_ge(acc_done, G + 2)

            def statistics(m, which, values, c, st_sem, mv_sem, ve_sem):
                for b in range(BLK):
                    dve.bn_stats(st_n[m % 2][:, which, b, :], values(b)).then_inc(st_sem, 1)
                if not (isinstance(c, int) and c < 2):
                    dve.wait_ge(ve_sem, c - 1)
                dve.wait_ge(st_sem, BLK * (c + 1))
                waits_end(dve)
                for b in range(BLK):
                    dve.bn_aggr(mv_n[m % 2][:, which, b, :], st_n[m % 2][:, which, b, :]).then_inc(mv_sem, 1)

            def norm(m, which, to, values, c, mv_sem, rs_sem, done):
                dve.wait_ge(mv_sem, BLK * (c + 1))
                dve.wait_ge(rs_sem, c + 1)
                for b in range(BLK):
                    dve.tensor_scalar(to[:, b, :], values(b), mv_n[m % 2][:, which, b, 0:1],
                                      rs_n[m % 2][:, which, b:b + 1], ALU.subtract, ALU.mult).then_inc(done, 1)

            def degree_columns(c, n0):
                return acc[:, KD, bass.ds(n0, CHUNK) if not isinstance(c, int) or c < C - 1 else slice((C - 1) * CHUNK, N)]

            def node_a(s):
                if at := s.at(1):
                    c, n0, m = at
                    dve.wait_ge(xt_in[m % 2], nth_in_slot(c, m % 2, 2, 16))
                    earlier(dve, a_f, c, 4)
                    dve.scalar_tensor_tensor(out=h_n[m], in0=xt_n[m % 2], scalar=2.0,
                                             in1=acc[:, 0:KD, bass.ds(n0, CHUNK)], op0=ALU.mult, op1=ALU.add
                                             ).then_inc(a_h, 1)
                if at := s.at(7):
                    c, n0, m = at
                    dve.wait_ge(a_y, c + 1)
                    stored(dve, y_out, c, m)
                    dve.tensor_tensor(y_n[m % 2], bank[6 + m % 2][:].rearrange("p (b d) -> p b d", d=D), row("b1m"), ALU.add
                                      ).then_inc(a_yr, 1)
                if at := s.at(4):
                    c, n0, m = at
                    dve.wait_ge(a_uT, c + 1)
                    statistics(m, 0, lambda b: bank[4][:, b * D:(b + 1) * D], c, a_st, a_mv, a_nb)
                if at := s.at(1):
                    c, n0, m = at
                    degree = degree_columns(c, n0)
                    width = degree.shape[-1]
                    dve.tensor_scalar(deg_n[:, 0:width], degree, 1.0, None, ALU.max).then_inc(a_d, 1)
                    dve.wait_ge(a_d, c + 1)
                    dve.reciprocal(rec_n[:, 0:width], deg_n[:, 0:width]).then_inc(a_id, 1)
                    dve.wait_ge(a_id, c + 1)
                    dve.scalar_tensor_tensor(out=degree, in0=degree, scalar=1.0, in1=rec_n[:, 0:width],
                                             op0=ALU.min, op1=ALU.mult).then_inc(a_rd, 1)
                if at := s.at(3):
                    c, n0, m = at
                    dve.wait_ge(a_z2, c + 1)
                    dve.wait_ge(a_h, c + 1)
                    dve.tensor_tensor(h_n[m], bank[3][:].rearrange("p (k n) -> p k n", k=KD), h_n[m], ALU.add
                                      ).then_inc(a_t, 1)
                if at := s.at(3):
                    c, n0, m = at
                    dve.wait_ge(a_t, c + 1)
                    dve.wait_ge(a_xc, c + 1)
                    earlier(dve, a_uT, c, 2)
                    for k in range(KD):
                        last = dve.scalar_tensor_tensor(out=u_n[m % 2][:, k, :], in0=h_n[m][:, k, :],
                                                        scalar=bn_s[:, 1, k:k + 1], in1=xc_n[m][:, k, :],
                                                        op0=ALU.mult, op1=ALU.add)
                    last.then_inc(a_u, 1)

            run_steps(dve, node_a, C, N, 7)

            dve.tensor_copy(w1m_hi[:], w1m_sb[:]).then_inc(w_split, 1)
            dve.wait_ge(w_split, 1)
            dve.tensor_tensor(w1m_lo[:], w1m_sb[:], w1m_hi[:].bitcast(F32), ALU.subtract).then_inc(w_split, 1)
            dve.wait_ge(w_high, KD + 2)
            for k in range(KD):
                dve.tensor_tensor(wmu_lo[:, k, :], bank[k][:], wmu_hi[:, k, :].bitcast(F32), ALU.subtract)
            dve.tensor_tensor(bmu_lo[:], bank[7][0:1, :], bmu_hi[:].bitcast(F32), ALU.subtract).then_inc(w_split, 1)
            dve.tensor_tensor(w2u_lo[:], w2u_sb[:], w2u_hi[:].bitcast(F32), ALU.subtract).then_inc(w_split, 1)
            dve.wait_ge(acc_zero, 4)

            def add_rows(g, slot, j):
                if j == 0:
                    dve.wait_ge(m_in[slot], nth_in_slot(g, slot, RING, 16 * TILES)
                                + 16 * TILES * slot_uses(G, slot, RING))
                dve.wait_ge(z_made, PAIRS * g + j + 1)
                v2 = m_sb[slot][:, 2 * j:2 * j + 2, :]
                dve.tensor_tensor(v2, z_bank(slot, j)[:].rearrange("p (t d) -> p t d", d=D), v2, ALU.add
                                  ).then_inc(added, 1)

            def eT_low_part(g, slot, j):
                dve.wait_ge(eT_high, PAIRS * g + j + 1)
                hi, lo = (part[j][:].rearrange("p (k t e) -> p k t e", k=KD, t=2) for part in (eT_hi, eT_lo))
                dve.tensor_tensor(lo, pair_of(eT_sb[slot % RING], j), hi.bitcast(F32), ALU.subtract
                                  ).then_inc(eT_low, 1)

            def second_pass(g, slot, low=True, ahead=True, sums=True):
                for j in range(PAIRS):
                    add_rows(g, slot, j)
                    if j == PAIRS - 1:
                        low_part(G, g, slot, 0)
                    elif low:
                        low_part(G, g - 1, slot - 1, j + 1)
                    if j == 1:
                        selection(G, g, slot)
                        if sums:
                            accumulate_group(G, g - 2, slot - 2, KD)
                    if ahead:
                        eT_low_part(g + 1, slot + 1, j)

            def second_pass_general(g, slot):
                for j in range(PAIRS):
                    add_rows(g, slot, j)
                    eT_low_part(g + 1, slot + 1, j)
                all_windows(G, g - 1, KD)

            for j in range(PAIRS):
                eT_low_part(0, 0, j)
            with dve.If(is_general > 0):
                for j in range(PAIRS):
                    add_rows(0, 0, j)
                    eT_low_part(1, 1, j)
                run_groups(dve, second_pass_general, 1, G - 1)
                for j in range(PAIRS):
                    add_rows(G - 1, (G - 1) % RING, j)
                all_windows(G, G - 2, KD)
                all_windows(G, G - 1, KD)
            with dve.Else():
                second_pass(0, 0, low=False, sums=False)
                second_pass(1, 1, sums=False)
                run_groups(dve, second_pass, 2, G - 1)
                second_pass(G - 1, (G - 1) % RING, ahead=False)
                for j in range(1, PAIRS):
                    low_part(G, G - 1, G - 1, j)
                for g in range(G - 2, G):
                    accumulate_group(G, g, g, KD)
            dve.wait_ge(acc_done, 2 * G + 2)

            def node_b(s):
                if at := s.at(0):
                    c, n0, m = at
                    earlier(dve, b_v, c, 2)
                    over_degree = acc[:, KD:KD + 1, bass.ds(n0, CHUNK)]
                    dve.tensor_scalar(some[m % 2], acc[0:1, KD, bass.ds(n0, CHUNK)], 0.0, None, ALU.is_gt)
                    dve.tensor_tensor(q_n[m % 2], acc[:, 0:KD, bass.ds(n0, CHUNK)],
                                      over_degree.broadcast_to([P, KD, CHUNK]), ALU.mult).then_inc(b_q, 1)
                if at := s.at(2):
                    c, n0, m = at
                    dve.wait_ge(b_gh, c + 1)
                    dve.wait_ge(b_g, c + 1)
                    for i in range(2):
                        last = dve.tensor_tensor(g_lo[m % 2][i][:], g_n[m % 2][:, i * KD:(i + 1) * KD, :]
                                                 .rearrange("p k n -> p (k n)"),
                                                 g_hi[m % 2][i][:].bitcast(F32), ALU.subtract)
                    last.then_inc(b_gl, 1)
                if at := s.at(4):
                    c, n0, m = at
                    dve.wait_ge(b_rT, c + 1)
                    statistics(m, 0, lambda b: bank[6 + m % 2][:, b * D:(b + 1) * D], c, b_st, b_mv, b_ve)
                if at := s.at(5):
                    c, n0, m = at
                    dve.wait_ge(b_s, c + 1)
                    statistics(m, 1, lambda b: n_n[m % 2][:, b, :], c, b_st2, b_mv2, b_nb)
                if at := s.at(3):
                    c, n0, m = at
                    dve.wait_ge(b_w, c + 1)
                    dve.wait_ge(x1T_in[m % 2], nth_in_slot(c, m % 2, 2, 16))
                    earlier(dve, b_rT, c, 2)
                    for k in range(KD):
                        last = dve.scalar_tensor_tensor(out=r_n[m % 2][:, k, :],
                                                        in0=bank[4 + m % 2][:, k * CHUNK:(k + 1) * CHUNK],
                                                        scalar=vec("b2u", k), in1=xt_n[m % 2][:, k, :],
                                                        op0=ALU.add, op1=ALU.add)
                    last.then_inc(b_r, 1)
                if at := s.at(4):
                    c, n0, m = at
                    if not (isinstance(c, int) and c < 2):
                        dve.wait_ge(b_o, BLK * (c - 1))
                    norm(m, 0, n_n[m % 2], lambda b: bank[6 + m % 2][:, b * D:(b + 1) * D], c, b_mv, b_rs, b_n)
                if at := s.at(0):
                    c, n0, m = at
                    dve.wait_ge(b_qh, c + 1)
                    dve.tensor_tensor(q_lo[m % 2][:], q_n[m % 2].rearrange("p k n -> p (k n)"),
                                      q_hi[m % 2][:].bitcast(F32), ALU.subtract).then_inc(b_ql, 1)

            run_steps(dve, node_b, C, N, 5)


def kernel(**inputs):
    import concourse.bacc as bacc
    from concourse.bass_utils import run_bass_kernel_spmd

    a = {k: np.asarray(v) for k, v in inputs.items()}
    names = {"L0_b1": "L0_gnn_b1", "L0_b2": "L0_gnn_b2", "b2m": "L1_gnn_b2m", "b2u": "L1_gnn_b2u"}
    per_feature = [a[names.get(n, "L0_gnn_" + n)] for n in VT[:-2]]
    per_feature += [a["L1_gnn_b1u"][0:D], a["L1_gnn_b1u"][D:2 * D]]
    arrays = {
        "x": a["x"], "xT": a["x"].T, "src": a["src"], "dst": a["dst"], "edge": a["edge_attr_256"],
        "edgeT": a["edge_attr_256"].T,
        "w1T": a["L0_gnn_W1"].T, "w2T": a["L0_gnn_W2"].T, "w1m": a["L1_gnn_W1m"], "w2mT": a["L1_gnn_W2m"].T,
        "w1u": a["L1_gnn_W1u"], "w2u": a["L1_gnn_W2u"],
        "vt": np.stack(per_feature).reshape(len(VT), KD, P).transpose(2, 0, 1),
        "vr": np.stack([a["L1_gnn_b1m"], a["L1_gnn_gamma"], a["L1_gnn_beta"]]),
    }
    arrays = {k: np.ascontiguousarray(v) for k, v in arrays.items()}
    nc = bacc.Bacc("TRN2", target_bir_lowering=False, num_devices=1)
    args = {k: nc.dram_tensor(f"in_{k}", v.shape, mybir.dt.from_np(v.dtype), kind="ExternalInput").ap()
            for k, v in arrays.items()}
    out = nc.dram_tensor("out", list(a["x"].shape), F32, kind="ExternalOutput").ap()
    build(nc, *args.values(), out)
    result = run_bass_kernel_spmd(nc, [{f"in_{k}": v for k, v in arrays.items()}], core_ids=[0])
    return result.results[0]["out"]
```
